# Optimizing a Trainium2 kernel written in Bass

```python
import numpy as np
import jax
import jax.numpy as jnp

def _softmax(x, axis=-1):
    return jax.nn.softmax(x, axis=axis)

def _gelu(x):
    return jax.nn.gelu(x, approximate=True)

def _silu(x):
    return jax.nn.silu(x)

def _sigmoid(x):
    return jax.nn.sigmoid(x)

def _layernorm(x, axis=-1, eps=1e-05):
    m = jnp.mean(x, axis=axis, keepdims=True)
    v = jnp.var(x, axis=axis, keepdims=True)
    return (x - m) / jnp.sqrt(v + eps)

def _scatter_add(tgt, idx, src, axis=0):
    return tgt.at[idx].add(src)

def _segment_sum(src, seg, n):
    return jax.ops.segment_sum(src, seg, n)
kernel_name = 'mk_vit_tower_d1_tok_img768_r4_54b3c9'

def setup_inputs(seed: int=0):
    np.random.seed(seed)
    _w = jnp.asarray

    def _rec_inputs():
        import jax
        import jax.numpy as jnp
        _rk = jax.random.key(seed)
        x = -0.000222058 + 0.999998 * jax.random.normal(jax.random.fold_in(_rk, 1), (16, 3, 128, 128), jnp.float32)
        return x
    x = _rec_inputs()

    def _L0_tok_setup():
        import jax, jax.numpy as jnp
        import numpy as np
        from jax import lax
        HIDDEN = 192
        C_IN = 3
        PATCH = 16
        SIDE = 32
        NUM_PATCHES = SIDE * SIDE

        def _position_ids(nb_h, nb_w):
            boundaries = np.arange(1.0 / SIDE, 1.0, 1.0 / SIDE, dtype=np.float32)
            frac_h = np.arange(0.0, 1.0 - 1e-06, 1.0 / nb_h, dtype=np.float32)
            frac_w = np.arange(0.0, 1.0 - 1e-06, 1.0 / nb_w, dtype=np.float32)
            bh = np.searchsorted(boundaries, frac_h, side='right')
            bw = np.searchsorted(boundaries, frac_w, side='right')
            return jnp.asarray((bh[:, None] * SIDE + bw).reshape(-1), dtype=jnp.int32)
        key = jax.random.key(seed)
        k1, k2, k3 = jax.random.split(key, 3)
        pixel_values = jax.random.normal(k1, (32, C_IN, 128, 128), dtype=jnp.float32)
        conv_w = jax.random.normal(k2, (HIDDEN, C_IN, PATCH, PATCH), dtype=jnp.float32) * 0.02
        conv_b = jnp.zeros((HIDDEN,), dtype=jnp.float32)
        pos_table = jax.random.normal(k3, (NUM_PATCHES, HIDDEN), dtype=jnp.float32) * 0.02
        return {'pixel_values': pixel_values, 'conv_w': conv_w, 'conv_b': conv_b, 'pos_table': pos_table}
    _L0_tok_all = _L0_tok_setup()
    _L0_tok_in = {k: v for k, v in _L0_tok_all.items() if k in ('conv_w', 'conv_b', 'pos_table')}
    del _L0_tok_all

    def _L0_attn_setup():
        import jax, jax.numpy as jnp
        import numpy as np
        B, T, D, H, MAX_REL = (4, 512, 192, 12, 128)
        HD = D // H
        key = jax.random.key(seed)
        ks = jax.random.split(key, 10)
        s = 0.02
        return {'x': jax.random.normal(ks[0], (B, T, D), dtype=jnp.float32), 'w_q': jax.random.normal(ks[1], (D, D), dtype=jnp.float32) * s, 'b_q': jnp.zeros((D,), dtype=jnp.float32), 'w_k': jax.random.normal(ks[2], (D, D), dtype=jnp.float32) * s, 'b_k': jnp.zeros((D,), dtype=jnp.float32), 'w_v': jax.random.normal(ks[3], (D, D), dtype=jnp.float32) * s, 'b_v': jnp.zeros((D,), dtype=jnp.float32), 'w_o': jax.random.normal(ks[4], (D, D), dtype=jnp.float32) * s, 'b_o': jnp.zeros((D,), dtype=jnp.float32), 'bias_table': jax.random.normal(ks[5], (2 * MAX_REL + 1, H), dtype=jnp.float32) * s}
    _L0_attn_all = _L0_attn_setup()
    _L0_attn_in = {k: v for k, v in _L0_attn_all.items() if k in ('w_q', 'b_q', 'w_k', 'b_k', 'w_v', 'b_v', 'w_o', 'b_o', 'bias_table')}
    del _L0_attn_all

    def _L0_ffn_setup():
        import jax, jax.numpy as jnp
        import numpy as np
        DEPTH = 11

        def _fff_forward(inputs, weights_in, weights_out, depth=DEPTH):
            B, S, _ = inputs.shape
            n_nodes = weights_in.shape[0]
            max_index = n_nodes - 1
            all_logits = jnp.einsum('bsd,nd->bsn', inputs, weights_in)

            def step(prev_idx, _):
                sel = jnp.clip(prev_idx, 0, max_index)
                logits = jnp.take_along_axis(all_logits, sel[..., None], axis=-1)[..., 0]
                new_idx = jnp.clip(2 * sel + 1 + (logits > 0).astype(sel.dtype), 0, max_index)
                return (new_idx, (logits, new_idx))
            idx0 = jnp.zeros((B, S), dtype=jnp.int32)
            _, (logits_seq, idx_seq) = jax.lax.scan(step, idx0, None, length=depth - 1)
            logits = jnp.concatenate([jnp.zeros((1, B, S), all_logits.dtype), logits_seq], axis=0)
            node_idx = jnp.concatenate([idx0[None], idx_seq], axis=0)
            act = jax.nn.gelu(logits, approximate=False)
            onehot = jax.nn.one_hot(node_idx, n_nodes, dtype=act.dtype)
            coeff = jnp.einsum('dbs,dbsn->bsn', act, onehot)
            return jnp.einsum('bsn,nd->bsd', coeff, weights_out)
        key = jax.random.key(seed)
        k1, k2, k3 = jax.random.split(key, 3)
        B, S, D = (4, 1024, 192)
        n_nodes = 2 * DEPTH - 1
        return {'inputs': jax.random.normal(k1, (B, S, D), dtype=jnp.float32), 'weights_in': jax.random.normal(k2, (n_nodes, D), dtype=jnp.float32), 'weights_out': jax.random.normal(k3, (n_nodes, D), dtype=jnp.float32)}
    _L0_ffn_all = _L0_ffn_setup()
    _L0_ffn_in = {k: v for k, v in _L0_ffn_all.items() if k in ('weights_in', 'weights_out')}
    del _L0_ffn_all
    return {'x': x, 'L0_tok_conv_w': _L0_tok_in['conv_w'], 'L0_tok_conv_b': _L0_tok_in['conv_b'], 'L0_tok_pos_table': _L0_tok_in['pos_table'], 'L0_attn_w_q': _L0_attn_in['w_q'], 'L0_attn_b_q': _L0_attn_in['b_q'], 'L0_attn_w_k': _L0_attn_in['w_k'], 'L0_attn_b_k': _L0_attn_in['b_k'], 'L0_attn_w_v': _L0_attn_in['w_v'], 'L0_attn_b_v': _L0_attn_in['b_v'], 'L0_attn_w_o': _L0_attn_in['w_o'], 'L0_attn_b_o': _L0_attn_in['b_o'], 'L0_attn_bias_table': _L0_attn_in['bias_table'], 'L0_ffn_weights_in': _L0_ffn_in['weights_in'], 'L0_ffn_weights_out': _L0_ffn_in['weights_out']}

def reference(x, L0_tok_conv_w, L0_tok_conv_b, L0_tok_pos_table, L0_attn_w_q, L0_attn_b_q, L0_attn_w_k, L0_attn_b_k, L0_attn_w_v, L0_attn_b_v, L0_attn_w_o, L0_attn_b_o, L0_attn_bias_table, L0_ffn_weights_in, L0_ffn_weights_out):
    import jax
    import jax.numpy as jnp

    def _L0_tok_ref(pixel_values, conv_w, conv_b, pos_table):
        import jax, jax.numpy as jnp
        import numpy as np
        from jax import lax
        HIDDEN = 192
        C_IN = 3
        PATCH = 16
        SIDE = 32
        NUM_PATCHES = SIDE * SIDE

        def _position_ids(nb_h, nb_w):
            boundaries = np.arange(1.0 / SIDE, 1.0, 1.0 / SIDE, dtype=np.float32)
            frac_h = np.arange(0.0, 1.0 - 1e-06, 1.0 / nb_h, dtype=np.float32)
            frac_w = np.arange(0.0, 1.0 - 1e-06, 1.0 / nb_w, dtype=np.float32)
            bh = np.searchsorted(boundaries, frac_h, side='right')
            bw = np.searchsorted(boundaries, frac_w, side='right')
            return jnp.asarray((bh[:, None] * SIDE + bw).reshape(-1), dtype=jnp.int32)
        B, _, H, W = pixel_values.shape
        nb_h, nb_w = (H // PATCH, W // PATCH)
        patches = lax.conv_general_dilated(pixel_values, conv_w, window_strides=(PATCH, PATCH), padding='VALID', dimension_numbers=('NCHW', 'OIHW', 'NCHW'))
        patches = patches + conv_b[None, :, None, None]
        embeddings = patches.reshape(B, HIDDEN, nb_h * nb_w).transpose(0, 2, 1)
        pos_ids = _position_ids(nb_h, nb_w)
        pos_emb = pos_table[pos_ids]
        return embeddings + pos_emb[None, :, :]

    def _L0_attn_ref(x, w_q, b_q, w_k, b_k, w_v, b_v, w_o, b_o, bias_table):
        import jax, jax.numpy as jnp
        import numpy as np
        B, T, D, H, MAX_REL = (4, 512, 192, 12, 128)
        HD = D // H
        Bn, Tn, Dn = x.shape
        max_rel = (bias_table.shape[0] - 1) // 2
        idx = jnp.arange(Tn)[:, None] - jnp.arange(Tn)[None, :]
        idx = jnp.clip(idx, -max_rel, max_rel) + max_rel
        mask = bias_table[idx].mean(-1)
        q = (x @ w_q.T + b_q).reshape(Bn, Tn, H, HD)
        k = (x @ w_k.T + b_k).reshape(Bn, Tn, H, HD)
        v = (x @ w_v.T + b_v).reshape(Bn, Tn, H, HD)
        scale = 1.0 / jnp.sqrt(jnp.asarray(HD, dtype=x.dtype))
        scores = jnp.einsum('bqhd,bkhd->bhqk', q, k) * scale + mask[None, None]
        attn = jax.nn.softmax(scores, axis=-1)
        ctx = jnp.einsum('bhqk,bkhd->bqhd', attn, v).reshape(Bn, Tn, Dn)
        return ctx @ w_o.T + b_o

    def _L0_ffn_ref(inputs, weights_in, weights_out):
        import jax, jax.numpy as jnp
        import numpy as np
        DEPTH = 11

        def _fff_forward(inputs, weights_in, weights_out, depth=DEPTH):
            B, S, _ = inputs.shape
            n_nodes = weights_in.shape[0]
            max_index = n_nodes - 1
            all_logits = jnp.einsum('bsd,nd->bsn', inputs, weights_in)

            def step(prev_idx, _):
                sel = jnp.clip(prev_idx, 0, max_index)
                logits = jnp.take_along_axis(all_logits, sel[..., None], axis=-1)[..., 0]
                new_idx = jnp.clip(2 * sel + 1 + (logits > 0).astype(sel.dtype), 0, max_index)
                return (new_idx, (logits, new_idx))
            idx0 = jnp.zeros((B, S), dtype=jnp.int32)
            _, (logits_seq, idx_seq) = jax.lax.scan(step, idx0, None, length=depth - 1)
            logits = jnp.concatenate([jnp.zeros((1, B, S), all_logits.dtype), logits_seq], axis=0)
            node_idx = jnp.concatenate([idx0[None], idx_seq], axis=0)
            act = jax.nn.gelu(logits, approximate=False)
            onehot = jax.nn.one_hot(node_idx, n_nodes, dtype=act.dtype)
            coeff = jnp.einsum('dbs,dbsn->bsn', act, onehot)
            return jnp.einsum('bsn,nd->bsd', coeff, weights_out)
        return _fff_forward(inputs, weights_in, weights_out)
    h = _L0_tok_ref(x, L0_tok_conv_w, L0_tok_conv_b, L0_tok_pos_table)
    h = h + _L0_attn_ref(_layernorm(h, axis=-1), L0_attn_w_q, L0_attn_b_q, L0_attn_w_k, L0_attn_b_k, L0_attn_w_v, L0_attn_b_v, L0_attn_w_o, L0_attn_b_o, L0_attn_bias_table)
    h = h + _L0_ffn_ref(_layernorm(h, axis=-1), L0_ffn_weights_in, L0_ffn_weights_out)
    return h

_drawn_inputs = setup_inputs


def setup_inputs(seed=0):
    import zlib

    import numpy as np

    out = dict(_drawn_inputs(seed))
    spreads = {'L0_tok_conv_b': (0.0, 0.1),
     'L0_attn_b_q': (0.0, 0.682),
     'L0_attn_b_k': (0.0, 2.0),
     'L0_attn_b_v': (0.0, 0.1),
     'L0_attn_b_o': (0.0, 0.1)}
    factors = {'L0_attn_w_q': 3.772, 'L0_attn_w_k': 4.059, 'L0_attn_bias_table': 33.596}
    for name, (base, spread) in spreads.items():
        noise = np.random.default_rng([zlib.crc32(name.encode()), seed]).standard_normal(out[name].shape)
        drawn = base * np.exp(spread * noise) if base else spread * noise
        out[name] = jnp.asarray(drawn.astype(out[name].dtype))
    for name, factor in factors.items():
        out[name] = (out[name] * factor).astype(out[name].dtype)
    return out
```

```python
import concourse.bass as bass
from concourse import mybir
from contextlib import ExitStack

B, C_IN, SIDE, PATCH = 16, 3, 128, 16
NP = SIDE // PATCH
T = NP * NP
D, H = 192, 12
HD = D // H
K_PIX = C_IN * PATCH * PATCH
POS_SIDE = 32
MAX_REL = 128
NODES = 21
DEPTH = 11
P = 128
NT = B * T // P
TPG = 2
NG = NT // TPG
GTOK = TPG * P
IPG = GTOK // T
KT = K_PIX // P
DB = D - P
HP = H // 2
VW = HD + 1
EPS = 1e-5
N_SETUP = 8

QK_W = 2 * D
W_V = QK_W
W_O = W_V + D
W_F = W_O + D
W_END = W_F + NODES

ROW_GROUP = [0, 1, 2, 3, 2, 3]
BANK_PAIRS = [[0], [1], [2, 4], [3, 5]]
BLOCKS = [(hp, t) for pairs in BANK_PAIRS for hp in pairs for t in range(TPG)]
BLOCK = {x: n for n, x in enumerate(BLOCKS)}
BANK_FIRST = [0, 2, 4, 8]
NBLK = len(BLOCKS)
PT_BANKS = NBLK // 4

PE_ORDER = [("embed", 0), ("embed", 1), ("xnT", 0), ("qk", 0), ("v", 0)]
for _g in range(NG):
    PE_ORDER.append(("scores", _g))
    if _g >= 1:
        PE_ORDER += [("ctxT", _g - 1), ("oproj", _g - 1)]
    if _g + 2 < NG:
        PE_ORDER.append(("embed", _g + 2))
    if _g + 1 < NG:
        PE_ORDER += [("xnT", _g + 1), ("qk", _g + 1), ("v", _g + 1)]
    if _g >= 1:
        PE_ORDER += [("xfT", _g - 1), ("logits", _g - 1)]
    PE_ORDER += [("probsT", _g), ("context", _g)]
PE_ORDER += [("ctxT", NG - 1), ("oproj", NG - 1)]
for _g in range(NG - 1):
    PE_ORDER += [("coefT", _g), ("leaf", _g)]
PE_ORDER += [("xfT", NG - 1), ("logits", NG - 1), ("coefT", NG - 1), ("leaf", NG - 1)]

STAGE_BANKS = {"scores": (0, 1, 2, 3), "probsT": (0, 1, 2), "embed": (4, 5), "oproj": (4, 5), "leaf": (4, 5),
               "context": (4, 5), "v": (4,), "xnT": (6,), "ctxT": (6,), "xfT": (6,), "coefT": (6,), "qk": (7, 6),
               "logits": (7,)}


def previous_user(stage, g, bank):
    at = PE_ORDER.index((stage, g))
    users = [x for x in PE_ORDER[:at] if bank in STAGE_BANKS[x[0]]]
    return users[-1] if users else None


def vit_block(nc, pixels, w_embed, w_proj_a, w_proj_b, w_leaf, pos_conv, bias_windows, constants, out):
    f32 = mybir.dt.float32
    ALU = mybir.AluOpType
    ACT = mybir.ActivationFunctionType
    AX = mybir.AxisListType

    ctx = ExitStack()
    with ctx:
        def sb(name, shape):
            return ctx.enter_context(nc.sbuf_tensor(name, shape, f32))

        def sem(name):
            return ctx.enter_context(nc.semaphore(name))

        pix = sb("pix", [P, NG, KT, GTOK])
        wemb = sb("wemb", [P, KT, D])
        wa = sb("wa", [P, W_END])
        wb = sb("wb", [DB + 1, W_END])
        wleaf = sb("wleaf", [NODES, D])
        posc = sb("posc", [P, 2, D])
        windows = sb("windows", [P, T, H])
        const = sb("const", [P, P + 2])
        ident = const[:, 0:P]
        head_of_pair = const[:, P:P + 2]
        pos = sb("pos", [P, D])
        mask = sb("mask", [P, T])
        mask_sum = sb("mask_sum", [P, T])
        neg_half = sb("neg_half", [P, TPG])
        h = sb("h", [P, NT, D])
        h2 = sb("h2", [P, NT, D])
        stats = sb("stats", [P, TPG, 6])
        mv = sb("mv", [P, 2, TPG, 2])
        var = sb("var", [P, 2, TPG])
        rstd = sb("rstd", [P, 2, TPG])
        stats_f = sb("stats_f", [P, TPG, 6])
        mv_f = sb("mv_f", [P, 2, TPG, 2])
        var_f = sb("var_f", [P, 2, TPG])
        rstd_f = sb("rstd_f", [P, 2, TPG])
        xn = sb("xn", [P, 2, TPG, D])
        xnT_a = sb("xnT_a", [P, 2, GTOK])
        xnT_b = sb("xnT_b", [DB + 1, 2, GTOK])
        q_a = sb("q_a", [P, 2, GTOK])
        q_b = sb("q_b", [P, 2, GTOK])
        k_a = sb("k_a", [P, 2, IPG, 2, T])
        k_b = sb("k_b", [P, 2, IPG, 2, T])
        v_bd = sb("v_bd", [P, 2, IPG, HP, 2, VW])
        s = sb("s", [P, 2, NBLK, 2 * T])
        smax = sb("smax", [P, 2, NBLK, 2])
        pT = sb("pT", [P, 2, NBLK, P])
        rden = sb("rden", [P, 2, TPG, H])
        cx = sb("cx", [P, 2, TPG, D])
        cxT_a = sb("cxT_a", [P, 2, GTOK])
        cxT_b = sb("cxT_b", [DB + 1, 2, GTOK])
        xf = sb("xf", [P, 2, TPG, D])
        xfT_a = sb("xfT_a", [P, 2, GTOK])
        xfT_b = sb("xfT_b", [DB + 1, 2, GTOK])
        logit = sb("logit", [P, NT, NODES])
        right_ = sb("right_", [P, NT, NODES])
        left_ = sb("left_", [P, NT, NODES])
        visit = sb("visit", [P, NT, NODES])
        steps = sb("steps", [P, NT, NODES])
        late = sb("late", [P, NT])
        gel = sb("gel", [P, NT, NODES])
        coef = sb("coef", [P, NT, NODES])
        tail = sb("tail", [P, NT, NODES])
        tail_sum = sb("tail_sum", [P, NT])
        cT = sb("cT", [NODES, 2, GTOK])
        y = sb("y", [P, NT, D])

        bank = [ctx.enter_context(nc.psum_tensor(f"bank{n}", [P, 512], f32)) for n in range(8)]

        ld_first = [sem(f"ld_first{n}") for n in range(2)]
        ld_pix = [sem(f"ld_pix{g}") for g in range(NG)]
        ld_const = sem("ld_const")
        ld_pos = sem("ld_pos")
        ld_win = sem("ld_win")
        ld_w = sem("ld_w")
        ld_leaf = sem("ld_leaf")
        stored = sem("stored")
        ready = {x: sem("pe_" + x) for x in STAGE_BANKS}
        setup = sem("setup")
        h_done = sem("h_done")
        mv_done = sem("mv_done")
        var_done = sem("var_done")
        rstd_done = sem("rstd_done")
        xn_done = sem("xn_done")
        xnT_done = sem("xnT_done")
        qk_done = sem("qk_done")
        k_done = sem("k_done")
        v_done = sem("v_done")
        masked = sem("masked")
        shifted = sem("shifted")
        exp_done = sem("exp_done")
        pT_done = sem("pT_done")
        cx_done = sem("cx_done")
        cxT_done = sem("cxT_done")
        h2_done = sem("h2_done")
        mvf_done = sem("mvf_done")
        varf_done = sem("varf_done")
        rstdf_done = sem("rstdf_done")
        xf_done = sem("xf_done")
        xfT_done = sem("xfT_done")
        logit_done = sem("logit_done")
        visit_done = sem("visit_done")
        gel_done = sem("gel_done")
        coef_done = sem("coef_done")
        cT_done = sem("cT_done")
        y_done = sem("y_done")
        dve_step = sem("dve_step")

        READ_BY_TILE = {"embed": h_done, "oproj": h2_done, "leaf": y_done, "context": cx_done}
        READ_BY_GROUP = {"v": (v_done, 2), "xnT": (xnT_done, 2), "ctxT": (cxT_done, 2), "xfT": (xfT_done, 2),
                         "coefT": (cT_done, 1), "logits": (logit_done, 1)}

        block = ctx.enter_context(nc.Block())

        @block.sync
        def _(sp):
            sp.dma_start(wemb[:, 0:3, :], w_embed[:, 0:3, :]).then_inc(ld_first[0], 16)
            sp.dma_start(pix[:, 0, 0:3, :], pixels[:, 0, 0:3, :]).then_inc(ld_first[0], 16)
            sp.dma_start(posc[:, :, :], pos_conv).then_inc(ld_pos, 16)
            sp.dma_start(pix[:, 1, :, :], pixels[:, 1, :, :]).then_inc(ld_pix[1], 16)
            sp.dma_start(wa[:, :], w_proj_a).then_inc(ld_w, 16)
            sp.dma_start(windows[:, :, :], bias_windows).then_inc(ld_win, 16)
            for g in range(2, NG):
                sp.dma_start(pix[:, g, :, :], pixels[:, g, :, :]).then_inc(ld_pix[g], 16)
            sp.dma_start(wleaf[:, :], w_leaf).then_inc(ld_leaf, 16)
            for g in range(NG):
                sp.wait_ge(y_done, TPG * (g + 1))
                for t in range(TPG * g, TPG * (g + 1)):
                    sp.dma_start(out[t, :, :], y[:, t, :]).then_inc(stored, 16)
            sp.wait_ge(stored, 16 * NT)

        @block.gpsimd
        def _(pool):
            n_set = 0
            for view, value in (
                (neg_half[:, :], -0.5),
                (xnT_b[DB:DB + 1, :, :], 1.0), (cxT_b[DB:DB + 1, :, :], 1.0), (xfT_b[DB:DB + 1, :, :], 1.0),
                (v_bd[0:T, :, :, :, 1, :], 0.0), (v_bd[T:P, :, :, :, 0, :], 0.0),
                (v_bd[0:T, :, :, :, 0, HD], 1.0), (v_bd[T:P, :, :, :, 1, HD], 1.0),
            ):
                if n_set:
                    pool.wait_ge(setup, n_set)
                nc.gpsimd.memset(view, value).then_inc(setup, 1)
                n_set += 1

            def root(g, mvs, vs, rs, seen, var_sem, rstd_sem):
                pool.wait_ge(seen, TPG * (g + 1))
                if g == 0:
                    pool.wait_ge(setup, N_SETUP)
                nc.gpsimd.tensor_scalar(vs[:, g % 2, :], mvs[:, g % 2, :, 1], EPS, 1.0, ALU.add, ALU.mult)\
                    .then_inc(var_sem, 1)
                pool.wait_ge(var_sem, g + 1)
                nc.gpsimd.tensor_tensor(rs[:, g % 2, :], vs[:, g % 2, :], neg_half[:, :], ALU.pow)\
                    .then_inc(rstd_sem, 1)

            root(0, mv, var, rstd, mv_done, var_done, rstd_done)
            root(1, mv, var, rstd, mv_done, var_done, rstd_done)
            for g in range(NG):
                if g >= 1:
                    root(g - 1, mv_f, var_f, rstd_f, mvf_done, varf_done, rstdf_done)
                if g + 2 < NG:
                    root(g + 2, mv, var, rstd, mv_done, var_done, rstd_done)
            root(NG - 1, mv_f, var_f, rstd_f, mvf_done, varf_done, rstdf_done)

        @block.scalar
        def _(act):
            act.dma_start(wemb[:, 3:KT, :], w_embed[:, 3:KT, :]).then_inc(ld_first[1], 16)
            act.dma_start(pix[:, 0, 3:KT, :], pixels[:, 0, 3:KT, :]).then_inc(ld_first[1], 16)
            act.dma_start(const[:, :], constants).then_inc(ld_const, 16)
            act.dma_start(wb[:, :], w_proj_b).then_inc(ld_w, 16)

            def copy_T(g, stage, dst_a, dst_b, done):
                act.wait_ge(ready[stage], g + 1)
                nc.scalar.activation(dst_a[:, g % 2, :], bank[6][:, 0:GTOK], ACT.Copy).then_inc(done, 1)
                nc.scalar.activation(dst_b[0:DB, g % 2, :], bank[6][0:DB, GTOK:2 * GTOK], ACT.Copy).then_inc(done, 1)

            def copy_qk(g):
                if g == 0:
                    act.wait_ge(ld_const, 16)
                act.wait_ge(ready["qk"], 2 * g + 1)
                scale = HD ** -0.5
                nc.scalar.activation(q_a[:, g % 2, :], bank[7][:, 0:GTOK], ACT.Copy, scale=scale).then_inc(qk_done, 1)
                nc.scalar.activation(q_b[T:P, g % 2, :], bank[7][0:T, GTOK:2 * GTOK], ACT.Copy, scale=scale)\
                    .then_inc(qk_done, 1)
                for j in range(2):
                    src = bank[7][T:P, GTOK:2 * GTOK].rearrange("p (i k) -> p i k", i=IPG)
                    nc.scalar.activation(k_b[T:P, g % 2, :, j, :], src, ACT.Copy,
                                         scale=head_of_pair[T:P, j:j + 1]).then_inc(qk_done, 1)

            def exps(g):
                for r in range(4):
                    act.wait_ge(shifted, 4 * g + r + 1)
                    at = BANK_FIRST[r]
                    p = s[:, g % 2, at:at + TPG * len(BANK_PAIRS[r]), :]
                    nc.scalar.activation(p, p, ACT.Exp).then_inc(exp_done, 1)

            def copy_pT(g):
                for r in range(PT_BANKS):
                    act.wait_ge(ready["probsT"], PT_BANKS * g + r + 1)
                    nc.scalar.activation(pT[:, g % 2, 4 * r:4 * r + 4, :].rearrange("p a b -> p (a b)"), bank[r][:, :],
                                         ACT.Copy).then_inc(pT_done, 1)

            act.wait_ge(setup, N_SETUP)
            copy_T(0, "xnT", xnT_a, xnT_b, xnT_done)
            copy_qk(0)
            for g in range(NG):
                if g >= 1:
                    copy_T(g - 1, "ctxT", cxT_a, cxT_b, cxT_done)
                exps(g)
                if g + 1 < NG:
                    copy_T(g + 1, "xnT", xnT_a, xnT_b, xnT_done)
                    copy_qk(g + 1)
                if g >= 1:
                    copy_T(g - 1, "xfT", xfT_a, xfT_b, xfT_done)
                copy_pT(g)

            def gelu(t0, t1, seen):
                act.wait_ge(logit_done, seen)
                nc.scalar.activation(gel[:, t0:t1, :], logit[:, t0:t1, :], ACT.Gelu).then_inc(gel_done, 1)

            def copy_cT(g):
                act.wait_ge(ready["coefT"], g + 1)
                nc.scalar.activation(cT[:, g % 2, :], bank[6][0:NODES, 0:GTOK], ACT.Copy).then_inc(cT_done, 1)

            gelu(0, NT - TPG, NG - 1)
            copy_T(NG - 1, "ctxT", cxT_a, cxT_b, cxT_done)
            for g in range(NG - 1):
                copy_cT(g)
            copy_T(NG - 1, "xfT", xfT_a, xfT_b, xfT_done)
            gelu(NT - TPG, NT, NG)
            copy_cT(NG - 1)

        @block.vector
        def _(dve):
            chain = [0]

            def link(ins):
                chain[0] += 1
                ins.then_inc(dve_step, 1)
                dve.wait_ge(dve_step, chain[0])

            def mark(ins):
                chain[0] += 1
                ins.then_inc(dve_step, 1)

            def hold():
                dve.wait_ge(dve_step, chain[0])

            dve.wait_ge(ld_pos, 16)
            link(nc.vector.tensor_tensor(pos[:, :], posc[:, 0, :], posc[:, 1, :], ALU.add))

            def moments(g, x, st, mvs, done):
                for t in range(TPG):
                    mark(nc.vector.bn_stats(st[:, t, :], x[:, TPG * g + t, :]))
                hold()
                for t in range(TPG):
                    nc.vector.bn_aggr(mvs[:, g % 2, t, :], st[:, t, :]).then_inc(done, 1)

            def normalise(g, x, mvs, rs, dst, rstd_sem, done):
                dve.wait_ge(rstd_sem, g + 1)
                for t in range(TPG):
                    nc.vector.tensor_scalar(dst[:, g % 2, t, :], x[:, TPG * g + t, :], mvs[:, g % 2, t, 0:1],
                                            rs[:, g % 2, t:t + 1], ALU.subtract, ALU.mult).then_inc(done, 1)

            def take_embed(g):
                for t in range(TPG):
                    dve.wait_ge(ready["embed"], TPG * g + t + 1)
                    nc.vector.tensor_tensor(h[:, TPG * g + t, :], bank[4 + t][:, 0:D], pos[:, :],
                                            ALU.add).then_inc(h_done, 1)
                dve.wait_ge(h_done, TPG * (g + 1))
                moments(g, h, stats, mv, mv_done)

            def take_k(g):
                dve.wait_ge(ready["qk"], 2 * g + 2)
                src = bank[6][:, 0:GTOK].rearrange("p (i k) -> p i k", i=IPG)
                for j in range(2):
                    nc.vector.tensor_scalar(k_a[:, g % 2, :, j, :], src, head_of_pair[:, j:j + 1], None, ALU.mult)\
                        .then_inc(k_done, 1)

            def take_v(g):
                dve.wait_ge(ready["v"], g + 1)
                for j in range(2):
                    rows = slice(j * T, (j + 1) * T)
                    src = bank[4][rows, 0:IPG * HP * HD].rearrange("p (i a d) -> p i a d", i=IPG, a=HP)
                    nc.vector.tensor_copy(v_bd[rows, g % 2, :, :, j, 0:HD], src).then_inc(v_done, 1)

            def softmax_shift(g):
                for r in range(4):
                    n = TPG * len(BANK_PAIRS[r])
                    at = BANK_FIRST[r]
                    rows = s[:, g % 2, at:at + n, :].rearrange("p a (j k) -> p (a j) k", j=2)
                    top = smax[:, g % 2, at:at + n, :].rearrange("p a j -> p (a j)")
                    dve.wait_ge(ready["scores"], 4 * g + r + 1)
                    nc.vector.tensor_tensor(rows, bank[r][:, 0:n * P].rearrange("p (u k) -> p u k", k=T),
                                            mask[:, :].unsqueeze(1).to_broadcast([P, 2 * n, T]),
                                            ALU.add).then_inc(masked, 1)
                    dve.wait_ge(masked, 4 * g + r + 1)
                    link(nc.vector.tensor_reduce(top, rows, AX.X, ALU.max))
                    nc.vector.tensor_tensor(rows, rows, top.unsqueeze(2).to_broadcast([P, 2 * n, T]),
                                            ALU.subtract).then_inc(shifted, 1)

            def take_context(g):
                for t in range(TPG):
                    dve.wait_ge(ready["context"], TPG * g + t + 1)
                    src = bank[4 + t][:, 0:H * VW].rearrange("p (a d) -> p a d", a=H)
                    link(nc.vector.reciprocal(rden[:, g % 2, t, :], src[:, :, HD]))
                    nc.vector.tensor_tensor(cx[:, g % 2, t, :].rearrange("p (a d) -> p a d", a=H), src[:, :, 0:HD],
                                            rden[:, g % 2, t, :].unsqueeze(2).to_broadcast([P, H, HD]),
                                            ALU.mult).then_inc(cx_done, 1)

            def take_oproj(g):
                for t in range(TPG):
                    dve.wait_ge(ready["oproj"], TPG * g + t + 1)
                    nc.vector.tensor_tensor(h2[:, TPG * g + t, :], bank[4 + t][:, 0:D],
                                            h[:, TPG * g + t, :], ALU.add).then_inc(h2_done, 1)
                dve.wait_ge(h2_done, TPG * (g + 1))
                moments(g, h2, stats_f, mv_f, mvf_done)

            def take_logits(g):
                ts = slice(TPG * g, TPG * (g + 1))
                dve.wait_ge(ready["logits"], g + 1)
                nc.vector.tensor_copy(logit[:, ts, :], bank[7][:, 0:TPG * NODES].rearrange("p (t n) -> p t n", t=TPG))\
                    .then_inc(logit_done, 1)
                dve.wait_ge(logit_done, g + 1)
                mark(nc.vector.tensor_single_scalar(right_[:, ts, :], logit[:, ts, :], 0.0, ALU.is_gt))
                mark(nc.vector.tensor_single_scalar(left_[:, ts, :], logit[:, ts, :], 0.0, ALU.is_le))
                hold()
                mark(nc.vector.tensor_copy(visit[:, ts, 1:2], left_[:, ts, 0:1]))
                mark(nc.vector.tensor_copy(visit[:, ts, 2:3], right_[:, ts, 0:1]))
                hold()
                for first, n in ((1, 2), (3, 4), (7, 3)):
                    src = slice(first, first + n)
                    mark(nc.vector.tensor_tensor(visit[:, ts, 2 * first + 1:2 * first + 2 * n:2], visit[:, ts, src],
                                                 left_[:, ts, src], ALU.mult))
                    mark(nc.vector.tensor_tensor(visit[:, ts, 2 * first + 2:2 * first + 2 * n + 1:2], visit[:, ts, src],
                                                 right_[:, ts, src], ALU.mult))
                    hold()
                mark(nc.vector.tensor_copy(steps[:, ts, 10:NODES - 1], visit[:, ts, 10:NODES - 1]))
                link(nc.vector.tensor_reduce(late[:, ts], visit[:, ts, 10:15], AX.X, ALU.add))
                nc.vector.scalar_tensor_tensor(steps[:, ts, NODES - 1], late[:, ts], float(DEPTH - 6),
                                               visit[:, ts, NODES - 1], ALU.add, ALU.add).then_inc(visit_done, 1)
                return ts

            def coefficients(g, gelus):
                ts = slice(TPG * g, TPG * (g + 1))
                dve.wait_ge(visit_done, g + 1)
                dve.wait_ge(gel_done, gelus)
                pairs = [P, TPG, 10, 2]
                mark(nc.vector.tensor_tensor(coef[:, ts, 1:NODES].rearrange("p t (n j) -> p t n j", j=2),
                                             visit[:, ts, 1:NODES].rearrange("p t (n j) -> p t n j", j=2),
                                             gel[:, ts, 0:10].unsqueeze(3).to_broadcast(pairs), ALU.mult))
                mark(nc.vector.memset(coef[:, ts, 0:1], 0.0))
                link(nc.vector.tensor_tensor(tail[:, ts, 10:NODES], steps[:, ts, 10:NODES], gel[:, ts, 10:NODES],
                                             ALU.mult))
                link(nc.vector.tensor_reduce(tail_sum[:, ts], tail[:, ts, 10:NODES], AX.X, ALU.add))
                nc.vector.tensor_tensor(coef[:, ts, NODES - 1], coef[:, ts, NODES - 1], tail_sum[:, ts], ALU.add)\
                    .then_inc(coef_done, 1)

            def take_leaf(g):
                for t in range(TPG):
                    dve.wait_ge(ready["leaf"], TPG * g + t + 1)
                    nc.vector.tensor_tensor(y[:, TPG * g + t, :], bank[4 + t][:, 0:D],
                                            h2[:, TPG * g + t, :], ALU.add).then_inc(y_done, 1)

            ln1 = (h, mv, rstd, xn, rstd_done, xn_done)
            ln2 = (h2, mv_f, rstd_f, xf, rstdf_done, xf_done)
            take_embed(0)
            dve.wait_ge(ld_win, 16)
            link(nc.vector.tensor_reduce(mask_sum[:, :], windows[:, :, :], AX.X, ALU.add))
            mark(nc.vector.tensor_single_scalar(mask[:, :], mask_sum[:, :], 1.0 / H, ALU.mult))
            normalise(0, *ln1)
            take_embed(1)
            dve.wait_ge(ld_const, 16)
            dve.wait_ge(setup, N_SETUP)
            take_k(0)
            take_v(0)
            normalise(1, *ln1)
            hold()
            for g in range(NG):
                softmax_shift(g)
                if g >= 1:
                    take_oproj(g - 1)
                if g + 2 < NG:
                    take_embed(g + 2)
                if g >= 1:
                    normalise(g - 1, *ln2)
                if g + 1 < NG:
                    take_k(g + 1)
                    take_v(g + 1)
                if g + 2 < NG:
                    normalise(g + 2, *ln1)
                if g >= 1:
                    take_logits(g - 1)
                take_context(g)
            for g in range(NG - 1):
                coefficients(g, 1)
            take_oproj(NG - 1)
            normalise(NG - 1, *ln2)
            for g in range(NG - 1):
                take_leaf(g)
            take_logits(NG - 1)
            coefficients(NG - 1, 2)
            take_leaf(NG - 1)

        @block.tensor
        def _(pe):
            def bank_free(stage, g, n):
                user = previous_user(stage, g, n)
                if user is None:
                    return
                name, ug = user
                if name == "scores":
                    pe.wait_ge(masked, 4 * ug + n + 1)
                elif name == "probsT":
                    pe.wait_ge(pT_done, PT_BANKS * ug + n + 1)
                elif name == "qk":
                    pe.wait_ge(*((qk_done, 4 * (ug + 1)) if n == 7 else (k_done, 2 * (ug + 1))))
                elif name in READ_BY_TILE:
                    pe.wait_ge(READ_BY_TILE[name], TPG * ug + n - 4 + 1)
                else:
                    reader, n_steps = READ_BY_GROUP[name]
                    pe.wait_ge(reader, n_steps * (ug + 1))

            def embed(g):
                for t in range(TPG):
                    bank_free("embed", g, 4 + t)
                    for k in range(KT):
                        if t == 0 and g == 0 and k % 3 == 0:
                            pe.wait_ge(ld_first[k // 3], 32)
                        elif t == 0 and g and k == 0:
                            pe.wait_ge(ld_pix[g], 16)
                        last = nc.tensor.matmul(bank[4 + t][:, 0:D], pix[:, g, k, t * P:(t + 1) * P],
                                                wemb[:, k, :], start=(k == 0), stop=(k == KT - 1))
                    last.then_inc(ready["embed"], 1)

            def transposes(g, stage, src, made):
                bank_free(stage, g, 6)
                if stage == "xnT" and g == 0:
                    pe.wait_ge(ld_const, 16)
                for t in range(TPG):
                    pe.wait_ge(made, TPG * g + t + 1)
                    nc.tensor.transpose(bank[6][:, t * P:(t + 1) * P], src[:, g % 2, t, 0:P], ident)
                    last = nc.tensor.transpose(bank[6][0:DB, GTOK + t * P:GTOK + (t + 1) * P],
                                               src[:, g % 2, t, P:D], ident)
                last.then_inc(ready[stage], 1)

            def qk(g):
                if g == 0:
                    pe.wait_ge(ld_w, 32)
                pe.wait_ge(xnT_done, 2 * (g + 1))
                bank_free("qk", g, 7)
                a, b = xnT_a[:, g % 2, :], xnT_b[:, g % 2, :]
                for n, col, at in ((7, 0, 0), (7, 2 * P, GTOK), (6, P, 0)):
                    if n == 6:
                        bank_free("qk", g, 6)
                    dst = bank[n][:, at:at + GTOK]
                    nc.tensor.matmul(dst, wa[:, col:col + P], a, start=True, stop=False)
                    last = nc.tensor.matmul(dst, wb[:, col:col + P], b, start=False, stop=True)
                    if at or n == 6:
                        last.then_inc(ready["qk"], 1)

            def v(g):
                bank_free("v", g, 4)
                for i in range(IPG):
                    for part, (w, x) in enumerate(((wa, xnT_a), (wb, xnT_b))):
                        for j in range(2):
                            col = W_V + j * HP * HD
                            last = nc.tensor.matmul(bank[4][j * T:(j + 1) * T, i * HP * HD:(i + 1) * HP * HD],
                                                    x[:, g % 2, i * T:(i + 1) * T], w[:, col:col + HP * HD],
                                                    start=(part == 0), stop=(part == 1))
                last.then_inc(ready["v"], 1)

            def scores(g):
                for r, pairs in enumerate(BANK_PAIRS):
                    bank_free("scores", g, r)
                    if r == 0:
                        pe.wait_ge(qk_done, 4 * (g + 1))
                        pe.wait_ge(k_done, 2 * (g + 1))
                    for hp in pairs:
                        q, k = (q_a, k_a) if hp < 4 else (q_b, k_b)
                        rows = slice(32 * ROW_GROUP[hp], 32 * ROW_GROUP[hp] + 32)
                        for t in range(TPG):
                            col = (BLOCK[hp, t] - BANK_FIRST[r]) * P
                            for i in range(2):
                                im = 2 * t + i
                                last = nc.tensor.matmul(bank[r][i * T:(i + 1) * T, col:col + P],
                                                        q[rows, g % 2, im * T:(im + 1) * T],
                                                        k[rows, g % 2, im, :, :].rearrange("p j k -> p (j k)"),
                                                        start=True, stop=True)
                    last.then_inc(ready["scores"], 1)

            def probsT(g):
                for r in range(PT_BANKS):
                    bank_free("probsT", g, r)
                    pe.wait_ge(exp_done, 4 * g + (2, 3, 4)[r])
                    for c in range(4):
                        last = nc.tensor.transpose(bank[r][:, c * P:(c + 1) * P], s[:, g % 2, 4 * r + c, :], ident)
                    last.then_inc(ready["probsT"], 1)

            def context(g):
                pe.wait_ge(v_done, 2 * (g + 1))
                pe.wait_ge(pT_done, PT_BANKS * (g + 1))
                for t in range(TPG):
                    bank_free("context", g, 4 + t)
                    for hp in range(HP):
                        for i in range(2):
                            at = hp * 2 * VW
                            last = nc.tensor.matmul(bank[4 + t][i * T:(i + 1) * T, at:at + 2 * VW],
                                                    pT[:, g % 2, BLOCK[hp, t], i * T:(i + 1) * T],
                                                    v_bd[:, g % 2, 2 * t + i, hp, :, :].rearrange("p j d -> p (j d)"),
                                                    start=True, stop=True)
                    last.then_inc(ready["context"], 1)

            def rows_times(g, stage, n, xa, xb, made, col, width):
                pe.wait_ge(made, 2 * (g + 1))
                for t in range(TPG):
                    if stage == "oproj":
                        bank_free(stage, g, n + t)
                        dst = bank[n + t][:, 0:width]
                    else:
                        if t == 0:
                            bank_free(stage, g, n)
                        dst = bank[n][:, t * width:(t + 1) * width]
                    nc.tensor.matmul(dst, xa[:, g % 2, t * P:(t + 1) * P], wa[:, col:col + width],
                                     start=True, stop=False)
                    last = nc.tensor.matmul(dst, xb[:, g % 2, t * P:(t + 1) * P], wb[:, col:col + width],
                                            start=False, stop=True)
                    if stage == "oproj":
                        last.then_inc(ready[stage], 1)
                if stage == "logits":
                    last.then_inc(ready[stage], 1)

            def coefT(g):
                bank_free("coefT", g, 6)
                pe.wait_ge(coef_done, g + 1)
                for t in range(TPG):
                    last = nc.tensor.transpose(bank[6][0:NODES, t * P:(t + 1) * P], coef[:, TPG * g + t, :], ident)
                last.then_inc(ready["coefT"], 1)

            def leaf(g):
                if g == 0:
                    pe.wait_ge(ld_leaf, 16)
                pe.wait_ge(cT_done, g + 1)
                for t in range(TPG):
                    bank_free("leaf", g, 4 + t)
                    nc.tensor.matmul(bank[4 + t][:, 0:D], cT[:, g % 2, t * P:(t + 1) * P], wleaf[:, :],
                                     start=True, stop=True).then_inc(ready["leaf"], 1)

            stages = {
                "embed": embed, "qk": qk, "v": v, "scores": scores, "probsT": probsT, "context": context,
                "coefT": coefT, "leaf": leaf,
                "xnT": lambda g: transposes(g, "xnT", xn, xn_done),
                "ctxT": lambda g: transposes(g, "ctxT", cx, cx_done),
                "xfT": lambda g: transposes(g, "xfT", xf, xf_done),
                "oproj": lambda g: rows_times(g, "oproj", 4, cxT_a, cxT_b, cxT_done, W_O, D),
                "logits": lambda g: rows_times(g, "logits", 7, xfT_a, xfT_b, xfT_done, W_F, NODES),
            }
            for stage, g in PE_ORDER:
                stages[stage](g)


def kernel(x, L0_tok_conv_w, L0_tok_conv_b, L0_tok_pos_table, L0_attn_w_q, L0_attn_b_q, L0_attn_w_k, L0_attn_b_k,
           L0_attn_w_v, L0_attn_b_v, L0_attn_w_o, L0_attn_b_o, L0_attn_bias_table, L0_ffn_weights_in,
           L0_ffn_weights_out):
    import numpy as np
    import concourse.bacc as bacc
    from concourse.bass_utils import run_bass_kernel_spmd as run

    px = np.asarray(x).reshape(B, C_IN, NP, PATCH, NP, PATCH).transpose(1, 3, 5, 0, 2, 4)
    px = px.reshape(KT, P, NG, GTOK).transpose(1, 2, 0, 3)
    we = np.asarray(L0_tok_conv_w).reshape(D, KT, P).transpose(2, 1, 0)
    def with_bias(w, b):
        return np.concatenate([np.asarray(w).T, np.asarray(b)[None, :]], axis=0)

    q, k, v, o = (with_bias(w, b) for w, b in ((L0_attn_w_q, L0_attn_b_q), (L0_attn_w_k, L0_attn_b_k),
                                               (L0_attn_w_v, L0_attn_b_v), (L0_attn_w_o, L0_attn_b_o)))
    f = with_bias(L0_ffn_weights_in, np.zeros(NODES, np.float32))
    v = v.reshape(D + 1, HP, 2, HD).transpose(0, 2, 1, 3).reshape(D + 1, D)
    w = np.concatenate([q[:, :P], k[:, :P], q[:, P:], k[:, P:], v, o, f], axis=1)
    step = POS_SIDE // NP
    pos = np.asarray(L0_tok_pos_table).reshape(NP, step, NP, step, D)[:, 0, :, 0].reshape(T, D)
    pos_conv = np.stack([np.concatenate([pos, pos]), np.broadcast_to(np.asarray(L0_tok_conv_b), (P, D))], axis=1)
    rel = np.arange(T)[:, None] - np.arange(T)[None, :] + MAX_REL
    win = np.asarray(L0_attn_bias_table)[rel]
    win = np.concatenate([win, win])
    head = (np.arange(P)[:, None] // HD) % 2 == np.arange(2)[None, :]
    constants = np.concatenate([np.eye(P), head], axis=1).astype(np.float32)

    host = dict(pixels=px, w_embed=we, w_proj_a=w[:P], w_proj_b=w[P:], w_leaf=np.asarray(L0_ffn_weights_out),
                pos_conv=pos_conv, bias_windows=win, constants=constants)
    nc = bacc.Bacc("TRN2", target_bir_lowering=False, num_devices=1)
    arrays, args = {}, []
    for name, a in host.items():
        arrays[name] = np.ascontiguousarray(a)
        args.append(nc.dram_tensor(name, a.shape, mybir.dt.from_np(a.dtype), kind="ExternalInput").ap())
    y = nc.dram_tensor("y_dram", (NT, P, D), mybir.dt.float32, kind="ExternalOutput").ap()
    vit_block(nc, *args, y)
    r = run(nc, [arrays], core_ids=[0])
    return r.results[0]["y_dram"].reshape(B, T, D)
```

```python
import concourse.bass as bass
from concourse import mybir
from contextlib import ExitStack

B, C_IN, SIDE, PATCH = 16, 3, 128, 16
NP = SIDE // PATCH
T = NP * NP
D, H = 192, 12
HD = D // H
K_PIX = C_IN * PATCH * PATCH
POS_SIDE = 32
MAX_REL = 128
NODES = 21
DEPTH = 11
STAY = NODES - 10
CK = NODES + STAY
P = 128
NT = B * T // P
TPG = 2
NG = NT // TPG
GTOK = TPG * P
IPG = GTOK // T
KT = K_PIX // P
DH = D // 2
HP = H // 2
VW = HD + 1
EPS = 1e-5
WARM = 2
N_SETUP = 12

QK_W = 2 * D
W_V = QK_W
W_O = W_V + D
W_F = W_O + D
W_END = W_F + NODES

ROW_GROUP = [0, 1, 2, 3, 2, 3]
BANK_PAIRS = [[0], [1], [2, 4], [3, 5]]
BLOCKS = [(hp, t) for pairs in BANK_PAIRS for hp in pairs for t in range(TPG)]
BLOCK = {x: n for n, x in enumerate(BLOCKS)}
BANK_FIRST = [0, 2, 4, 8]
NBLK = len(BLOCKS)
PT_BANKS = NBLK // 4

PE_ORDER = (
    [("embed", 0), ("embed", 1), ("embed", 2), ("xnT", 0), ("xnT", 1), ("embed", 3), ("qk", 0), ("v", 0)]
    + [("scores", 0), ("scores", 1), ("embed", 4), ("scores", 2), ("xnT", 2), ("xnT", 3), ("scores", 3), ("qk", 1),
       ("embed", 5), ("probsT", 0), ("v", 1), ("context", 0), ("embed", 6)]
    + [("scores", 4), ("ctxT", 0), ("scores", 5), ("ctxT", 1), ("scores", 6), ("oproj", 0), ("scores", 7),
       ("oproj", 1), ("xnT", 4), ("xnT", 5), ("qk", 2), ("probsT", 1), ("xfT", 0), ("xfT", 1), ("v", 2),
       ("context", 1), ("embed", 7)]
    + [("scores", 8), ("ctxT", 2), ("scores", 9), ("ctxT", 3), ("scores", 10), ("oproj", 2), ("scores", 11),
       ("oproj", 3), ("logits", 0), ("xnT", 6), ("xnT", 7), ("qk", 3), ("probsT", 2), ("xfT", 2), ("xfT", 3),
       ("context", 2), ("v", 3)]
    + [("scores", 12), ("ctxT", 4), ("scores", 13), ("ctxT", 5), ("scores", 14), ("oproj", 4), ("scores", 15),
       ("oproj", 5), ("logits", 1), ("coefT", 0), ("leaf", 0), ("leaf", 1), ("probsT", 3), ("xfT", 4), ("xfT", 5),
       ("context", 3)]
    + [("logits", 2), ("ctxT", 6), ("ctxT", 7), ("coefT", 1), ("oproj", 6), ("oproj", 7), ("leaf", 2),
       ("leaf", 3), ("coefT", 2), ("leaf", 4), ("xfT", 6), ("leaf", 5),
       ("xfT", 7), ("logits", 3), ("coefT", 3), ("leaf", 6), ("leaf", 7)]
)


def banks_of(stage, n):
    if stage == "embed":
        return (4 + n % TPG if n < 6 else 7,)
    if stage == "leaf":
        return (4 + n if n < TPG else n % 4,)
    if stage in ("xnT", "ctxT", "xfT"):
        return (6 + n % TPG,)
    if stage == "scores":
        return (n % 4,)
    return {"probsT": (0, 1, 2), "context": (4, 5), "oproj": (4 + n % TPG,), "v": (3,), "coefT": (6,), "qk": (7, 6),
            "logits": (6,)}[stage]


def previous_user(stage, n, bank):
    at = PE_ORDER.index((stage, n))
    users = [x for x in PE_ORDER[:at] if bank in banks_of(*x)]
    return users[-1] if users else None


def vit_block(nc, pixels, w_embed, w_proj, w_leaf, pos_conv, bias_windows, constants, out):
    f32 = mybir.dt.float32
    ALU = mybir.AluOpType
    ACT = mybir.ActivationFunctionType
    AX = mybir.AxisListType

    ctx = ExitStack()
    with ctx:
        def sb(name, shape):
            return ctx.enter_context(nc.sbuf_tensor(name, shape, f32))

        def sem(name):
            return ctx.enter_context(nc.semaphore(name))

        pix = sb("pix", [P, NG, KT, GTOK])
        wemb = sb("wemb", [P, KT, D])
        w = sb("w", [P, 2, W_END])
        wleaf = sb("wleaf", [P, D])
        posc = sb("posc", [P, 2, D])
        windows = sb("windows", [P, T, H])
        const = sb("const", [P, P + 2])
        ident = const[:, 0:P]
        head_of_pair = const[:, P:P + 2]
        pos = sb("pos", [P, D])
        mask = sb("mask", [P, T])
        mask_sum = sb("mask_sum", [P, T])
        warm = sb("warm", [P, 512])
        neg_half = sb("neg_half", [P, 1])
        h = sb("h", [P, NT, D])
        h2 = sb("h2", [P, NT, D])
        stats = sb("stats", [P, NT, 6])
        mv = sb("mv", [P, NT, 2])
        var = sb("var", [P, NT])
        rstd = sb("rstd", [P, NT])
        stats_f = sb("stats_f", [P, NT, 6])
        mv_f = sb("mv_f", [P, NT, 2])
        var_f = sb("var_f", [P, NT])
        rstd_f = sb("rstd_f", [P, NT])
        xn = sb("xn", [P, 4, D])
        xnT = sb("xnT", [P, 2, 2, GTOK])
        q_a = sb("q_a", [P, 2, GTOK])
        q_b = sb("q_b", [P, 2, GTOK])
        k_a = sb("k_a", [P, 2, IPG, 2, T])
        k_b = sb("k_b", [P, 2, IPG, 2, T])
        v_bd = sb("v_bd", [P, 2, IPG, HP, 2, VW])
        s = sb("s", [P, 2, NBLK, 2 * T])
        smax = sb("smax", [P, 2, NBLK, 2])
        pT = sb("pT", [P, 2, NBLK, P])
        rden = sb("rden", [P, 4, H])
        cx = sb("cx", [P, 4, D])
        cxT = sb("cxT", [P, 2, 2, GTOK])
        xf = sb("xf", [P, 4, D])
        xfT = sb("xfT", [P, 2, 2, GTOK])
        logit = sb("logit", [P, NT, NODES])
        turn = sb("turn", [P, NT, NODES, 2])
        visit = sb("visit", [P, NT, NODES])
        steps = sb("steps", [P, NT, NODES])
        late = sb("late", [P, NT])
        gel = sb("gel", [P, NT, NODES])
        coef = sb("coef", [P, NT, CK])
        cT = sb("cT", [P, 2, GTOK])
        y = sb("y", [P, NT, D])

        bank = [ctx.enter_context(nc.psum_tensor(f"bank{n}", [P, 512], f32)) for n in range(8)]

        ld_first = [sem(f"ld_first{n}") for n in range(KT // 2)]
        ld_pix = [sem(f"ld_pix{g}") for g in range(NG)]
        ld_const = sem("ld_const")
        warm_set = sem("warm_set")
        ld_pos = sem("ld_pos")
        ld_win = sem("ld_win")
        ld_w = sem("ld_w")
        ld_leaf = sem("ld_leaf")
        stored = sem("stored")
        ready = {x: sem("pe_" + x) for x in sorted({x[0] for x in PE_ORDER})}
        setup = sem("setup")
        h_done = sem("h_done")
        var_done = sem("var_done")
        rstd_done = sem("rstd_done")
        xn_done = sem("xn_done")
        xnT_done = sem("xnT_done")
        qk_done = sem("qk_done")
        k_done = sem("k_done")
        v_done = sem("v_done")
        masked = sem("masked")
        max_done = sem("max_done")
        shifted = sem("shifted")
        exp_done = sem("exp_done")
        pT_done = sem("pT_done")
        cx_done = sem("cx_done")
        cxT_done = sem("cxT_done")
        h2_done = sem("h2_done")
        varf_done = sem("varf_done")
        rstdf_done = sem("rstdf_done")
        xf_done = sem("xf_done")
        xfT_done = sem("xfT_done")
        logit_done = sem("logit_done")
        visit_done = sem("visit_done")
        gel_done = sem("gel_done")
        coef_done = sem("coef_done")
        cT_done = sem("cT_done")
        y_done = sem("y_done")
        dve_step = sem("dve_step")

        READ_BY_TILE = {"embed": h_done, "xnT": xnT_done, "ctxT": cxT_done, "oproj": h2_done, "xfT": xfT_done,
                        "leaf": y_done}
        READ_BY_GROUP = {"v": (v_done, 2), "coefT": (cT_done, 1), "logits": (logit_done, 1)}

        def score_rows(g, r):
            n = TPG * len(BANK_PAIRS[r])
            at = BANK_FIRST[r]
            return (s[:, g % 2, at:at + n, :].rearrange("p a (j k) -> p (a j) k", j=2),
                    smax[:, g % 2, at:at + n, :].rearrange("p a j -> p (a j)"), 2 * n)

        block = ctx.enter_context(nc.Block())

        @block.sync
        def _(sp):
            for n in range(KT // 2):
                sp.dma_start(wemb[:, 2 * n:2 * n + 2, :], w_embed[:, 2 * n:2 * n + 2, :]).then_inc(ld_first[n], 16)
            sp.dma_start(posc[:, :, :], pos_conv).then_inc(ld_pos, 16)
            sp.dma_start(pix[:, 1, :, :], pixels[:, 1, :, :]).then_inc(ld_pix[1], 16)
            sp.dma_start(w[:, :, :], w_proj).then_inc(ld_w, 16)
            sp.dma_start(windows[:, :, :], bias_windows).then_inc(ld_win, 16)
            for g in range(2, NG):
                sp.dma_start(pix[:, g, :, :], pixels[:, g, :, :]).then_inc(ld_pix[g], 16)
            sp.dma_start(wleaf[:, :], w_leaf).then_inc(ld_leaf, 16)
            for t in range(NT):
                sp.wait_ge(y_done, t + 1)
                sp.dma_start(out[t, :, :], y[:, t, :]).then_inc(stored, 16)
            sp.wait_ge(stored, 16 * NT)

        @block.gpsimd
        def _(pool):
            n_set = 0
            for view, value in (
                (neg_half[:, :], -0.5),
                (cT[:, :, :], 0.0), (xnT[DH:P, :, :, :], 0.0), (cxT[DH:P, :, :, :], 0.0), (xfT[DH:P, :, :, :], 0.0),
                (xnT[DH:DH + 1, :, 1, :], 1.0), (cxT[DH:DH + 1, :, 1, :], 1.0), (xfT[DH:DH + 1, :, 1, :], 1.0),
                (v_bd[0:T, :, :, :, 1, :], 0.0), (v_bd[T:P, :, :, :, 0, :], 0.0),
                (v_bd[0:T, :, :, :, 0, HD], 1.0), (v_bd[T:P, :, :, :, 1, HD], 1.0),
            ):
                if n_set:
                    pool.wait_ge(setup, n_set)
                nc.gpsimd.memset(view, value).then_inc(setup, 1)
                n_set += 1

            def root(t, vs, rs, var_sem, rstd_sem):
                pool.wait_ge(var_sem, t + 1)
                if t == 0:
                    pool.wait_ge(setup, N_SETUP)
                nc.gpsimd.tensor_tensor(rs[:, t:t + 1], vs[:, t:t + 1], neg_half[:, :], ALU.pow).then_inc(rstd_sem, 1)

            def shift(n):
                g, r = divmod(n, 4)
                rows, top, units = score_rows(g, r)
                pool.wait_ge(max_done, n + 1)
                nc.gpsimd.tensor_tensor(rows, rows, top.unsqueeze(2).to_broadcast([P, units, T]), ALU.subtract)\
                    .then_inc(shifted, 1)

            ln1 = (var, rstd, var_done, rstd_done)
            ln2 = (var_f, rstd_f, varf_done, rstdf_done)
            for t in range(4):
                root(t, *ln1)
            for r in range(4):
                shift(r)
            root(4, *ln1)
            root(5, *ln1)
            root(6, *ln1)
            for r in range(4):
                shift(4 + r)
            root(0, *ln2)
            root(1, *ln2)
            root(7, *ln1)
            for r in range(4):
                shift(8 + r)
            root(2, *ln2)
            root(3, *ln2)
            for r in range(4):
                shift(12 + r)
            for t in range(4, NT):
                root(t, *ln2)

        @block.scalar
        def _(act):
            for n in range(KT // 2):
                act.dma_start(pix[:, 0, 2 * n:2 * n + 2, :], pixels[:, 0, 2 * n:2 * n + 2, :])\
                    .then_inc(ld_first[n], 16)
            act.dma_start(const[:, :], constants).then_inc(ld_const, 16)

            def copy_T(t, stage, dst, done):
                g, half = divmod(t, TPG)
                act.wait_ge(ready[stage], t + 1)
                nc.scalar.activation(dst[0:DH, g % 2, :, half * P:(half + 1) * P],
                                     bank[6 + half][0:DH, 0:2 * P].rearrange("p (j n) -> p j n", j=2),
                                     ACT.Copy).then_inc(done, 1)

            def copy_qk(g):
                if g == 0:
                    act.wait_ge(ld_const, 16)
                act.wait_ge(ready["qk"], 2 * g + 1)
                scale = HD ** -0.5
                nc.scalar.activation(q_a[:, g % 2, :], bank[7][:, 0:GTOK], ACT.Copy, scale=scale).then_inc(qk_done, 1)
                nc.scalar.activation(q_b[T:P, g % 2, :], bank[7][0:T, GTOK:2 * GTOK], ACT.Copy, scale=scale)\
                    .then_inc(qk_done, 1)
                for j in range(2):
                    src = bank[7][T:P, GTOK:2 * GTOK].rearrange("p (i k) -> p i k", i=IPG)
                    nc.scalar.activation(k_b[T:P, g % 2, :, j, :], src, ACT.Copy,
                                         scale=head_of_pair[T:P, j:j + 1]).then_inc(qk_done, 1)

            def exp(n):
                g, r = divmod(n, 4)
                rows, _, _ = score_rows(g, r)
                act.wait_ge(shifted, n + 1)
                nc.scalar.activation(rows, rows, ACT.Exp).then_inc(exp_done, 1)

            def copy_pT(g):
                for r in range(PT_BANKS):
                    act.wait_ge(ready["probsT"], PT_BANKS * g + r + 1)
                    nc.scalar.activation(pT[:, g % 2, 4 * r:4 * r + 4, :].rearrange("p a b -> p (a b)"), bank[r][:, :],
                                         ACT.Copy).then_inc(pT_done, 1)

            act.wait_ge(setup, N_SETUP)
            def copy_xnT(t):
                copy_T(t, "xnT", xnT, xnT_done)

            def copy_ctxT(t):
                copy_T(t, "ctxT", cxT, cxT_done)

            def copy_xfT(t):
                copy_T(t, "xfT", xfT, xfT_done)

            def gelu(t0, t1):
                act.wait_ge(logit_done, t1 // TPG)
                nc.scalar.activation(gel[:, t0:t1, :], logit[:, t0:t1, :], ACT.Gelu).then_inc(gel_done, 1)

            def copy_cT(g):
                act.wait_ge(ready["coefT"], g + 1)
                nc.scalar.activation(cT[0:CK, g % 2, :], bank[6][0:CK, 0:GTOK], ACT.Copy).then_inc(cT_done, 1)

            copy_xnT(0)
            copy_xnT(1)
            copy_qk(0)
            exp(0)
            exp(1)
            copy_xnT(2)
            copy_xnT(3)
            exp(2)
            exp(3)
            copy_qk(1)
            copy_pT(0)
            exp(4)
            copy_ctxT(0)
            copy_ctxT(1)
            exp(5)
            exp(6)
            exp(7)
            copy_xnT(4)
            copy_xnT(5)
            copy_qk(2)
            copy_pT(1)
            copy_xfT(0)
            copy_xfT(1)
            copy_ctxT(2)
            exp(8)
            copy_ctxT(3)
            exp(9)
            exp(10)
            exp(11)
            copy_xnT(6)
            copy_xnT(7)
            copy_qk(3)
            copy_pT(2)
            gelu(0, TPG)
            copy_xfT(2)
            copy_xfT(3)
            copy_ctxT(4)
            exp(12)
            copy_ctxT(5)
            exp(13)
            exp(14)
            exp(15)
            copy_cT(0)
            copy_pT(3)
            gelu(TPG, 2 * TPG)
            copy_xfT(4)
            copy_xfT(5)
            copy_ctxT(6)
            copy_ctxT(7)
            copy_cT(1)
            gelu(2 * TPG, 3 * TPG)
            copy_cT(2)
            copy_xfT(6)
            copy_xfT(7)
            gelu(3 * TPG, NT)
            copy_cT(3)

        @block.vector
        def _(dve):
            chain = [0]

            def link(ins):
                chain[0] += 1
                ins.then_inc(dve_step, 1)
                dve.wait_ge(dve_step, chain[0])

            def mark(ins):
                chain[0] += 1
                ins.then_inc(dve_step, 1)

            def hold():
                dve.wait_ge(dve_step, chain[0])

            nc.vector.memset(warm[:, :], 0.0).then_inc(warm_set, 1)
            mark(nc.vector.memset(coef[:, :, 0:1], 0.0))
            dve.wait_ge(ld_pos, 16)
            link(nc.vector.tensor_tensor(pos[:, :], posc[:, 0, :], posc[:, 1, :], ALU.add))

            def variance(t, x, st, mvs, vs, done):
                link(nc.vector.bn_stats(st[:, t, :], x[:, t, :]))
                link(nc.vector.bn_aggr(mvs[:, t, :], st[:, t, :]))
                nc.vector.tensor_single_scalar(vs[:, t:t + 1], mvs[:, t, 1:2], EPS, ALU.add).then_inc(done, 1)

            def normalise(t, x, mvs, rs, dst, rstd_sem, done):
                dve.wait_ge(rstd_sem, t + 1)
                nc.vector.tensor_scalar(dst[:, t % 4, :], x[:, t, :], mvs[:, t, 0:1], rs[:, t:t + 1],
                                        ALU.subtract, ALU.mult).then_inc(done, 1)

            def take_embed(t):
                dve.wait_ge(ready["embed"], t + 1)
                nc.vector.tensor_tensor(h[:, t, :], bank[banks_of("embed", t)[0]][:, 0:D], pos[:, :], ALU.add).then_inc(h_done, 1)
                dve.wait_ge(h_done, t + 1)
                variance(t, h, stats, mv, var, var_done)

            def take_k(g):
                dve.wait_ge(ready["qk"], 2 * g + 2)
                src = bank[6][:, 0:GTOK].rearrange("p (i k) -> p i k", i=IPG)
                for j in range(2):
                    nc.vector.tensor_scalar(k_a[:, g % 2, :, j, :], src, head_of_pair[:, j:j + 1], None, ALU.mult)\
                        .then_inc(k_done, 1)

            def take_v(g):
                dve.wait_ge(ready["v"], g + 1)
                for j in range(2):
                    rows = slice(j * T, (j + 1) * T)
                    src = bank[banks_of("v", g)[0]][rows, 0:IPG * HP * HD].rearrange("p (i a d) -> p i a d", i=IPG, a=HP)
                    nc.vector.tensor_copy(v_bd[rows, g % 2, :, :, j, 0:HD], src).then_inc(v_done, 1)

            def mask_and_max(n):
                g, r = divmod(n, 4)
                rows, top, units = score_rows(g, r)
                dve.wait_ge(ready["scores"], n + 1)
                nc.vector.tensor_tensor(rows, bank[r][:, 0:units * T].rearrange("p (u k) -> p u k", k=T),
                                        mask[:, :].unsqueeze(1).to_broadcast([P, units, T]), ALU.add)\
                    .then_inc(masked, 1)
                dve.wait_ge(masked, n + 1)
                nc.vector.tensor_reduce(top, rows, AX.X, ALU.max).then_inc(max_done, 1)

            def take_context(g):
                for t in range(TPG):
                    dve.wait_ge(ready["context"], TPG * g + t + 1)
                    src = bank[4 + t][:, 0:H * VW].rearrange("p (a d) -> p a d", a=H)
                    n = (TPG * g + t) % 4
                    link(nc.vector.reciprocal(rden[:, n, :], src[:, :, HD]))
                    nc.vector.tensor_tensor(cx[:, n, :].rearrange("p (a d) -> p a d", a=H), src[:, :, 0:HD],
                                            rden[:, n, :].unsqueeze(2).to_broadcast([P, H, HD]),
                                            ALU.mult).then_inc(cx_done, 1)

            def take_oproj(t):
                dve.wait_ge(ready["oproj"], t + 1)
                nc.vector.tensor_tensor(h2[:, t, :], bank[4 + t % TPG][:, 0:D], h[:, t, :], ALU.add)\
                    .then_inc(h2_done, 1)
                dve.wait_ge(h2_done, t + 1)
                variance(t, h2, stats_f, mv_f, var_f, varf_done)

            def take_logits(g):
                ts = slice(TPG * g, TPG * (g + 1))
                dve.wait_ge(ready["logits"], g + 1)
                nc.vector.tensor_copy(logit[:, ts, :], bank[6][:, 0:TPG * NODES].rearrange("p (t n) -> p t n", t=TPG))\
                    .then_inc(logit_done, 1)

            def walk(g):
                ts = slice(TPG * g, TPG * (g + 1))
                dve.wait_ge(logit_done, g + 1)
                mark(nc.vector.tensor_single_scalar(turn[:, ts, :, 0], logit[:, ts, :], 0.0, ALU.is_le))
                mark(nc.vector.tensor_single_scalar(turn[:, ts, :, 1], logit[:, ts, :], 0.0, ALU.is_gt))
                hold()
                for first, n in ((1, 2), (3, 4), (7, 3)):
                    parents = turn[:, ts, 0, :] if first == 1 else visit[:, ts, first:first + n]
                    children = visit[:, ts, 2 * first + 1:2 * first + 1 + 2 * n].rearrange("p t (n j) -> p t n j", j=2)
                    mark(nc.vector.tensor_tensor(children, turn[:, ts, first:first + n, :],
                                                 parents.unsqueeze(3).to_broadcast([P, TPG, n, 2]), ALU.mult))
                    if first == 1:
                        mark(nc.vector.tensor_copy(visit[:, ts, 1:3], turn[:, ts, 0, :]))
                    hold()
                mark(nc.vector.tensor_copy(steps[:, ts, 10:NODES - 1], visit[:, ts, 10:NODES - 1]))
                link(nc.vector.tensor_reduce(late[:, ts], visit[:, ts, 10:15], AX.X, ALU.add))
                nc.vector.scalar_tensor_tensor(steps[:, ts, NODES - 1], late[:, ts], float(DEPTH - 6),
                                               visit[:, ts, NODES - 1], ALU.add, ALU.add).then_inc(visit_done, 1)

            def coefficients(g, gelus):
                ts = slice(TPG * g, TPG * (g + 1))
                dve.wait_ge(visit_done, g + 1)
                dve.wait_ge(gel_done, gelus)
                pairs = [P, TPG, 10, 2]
                mark(nc.vector.tensor_tensor(coef[:, ts, 1:NODES].rearrange("p t (n j) -> p t n j", j=2),
                                             visit[:, ts, 1:NODES].rearrange("p t (n j) -> p t n j", j=2),
                                             gel[:, ts, 0:10].unsqueeze(3).to_broadcast(pairs), ALU.mult))
                nc.vector.tensor_tensor(coef[:, ts, NODES:CK], steps[:, ts, 10:NODES], gel[:, ts, 10:NODES],
                                        ALU.mult).then_inc(coef_done, 1)

            def take_leaf(t):
                dve.wait_ge(ready["leaf"], t + 1)
                nc.vector.tensor_tensor(y[:, t, :], bank[banks_of("leaf", t)[0]][:, 0:D], h2[:, t, :], ALU.add)\
                    .then_inc(y_done, 1)

            ln1 = (h, mv, rstd, xn, rstd_done, xn_done)
            ln2 = (h2, mv_f, rstd_f, xf, rstdf_done, xf_done)
            take_embed(0)
            take_embed(1)
            dve.wait_ge(ld_win, 16)
            link(nc.vector.tensor_reduce(mask_sum[:, :], windows[:, :, :], AX.X, ALU.add))
            mark(nc.vector.tensor_single_scalar(mask[:, :], mask_sum[:, :], 1.0 / H, ALU.mult))
            normalise(0, *ln1)
            normalise(1, *ln1)
            take_embed(2)
            take_embed(3)
            dve.wait_ge(ld_const, 16)
            dve.wait_ge(setup, N_SETUP)
            take_k(0)
            normalise(2, *ln1)
            normalise(3, *ln1)
            take_v(0)
            hold()
            for r in range(4):
                mask_and_max(r)
            take_embed(4)
            take_k(1)
            take_embed(5)
            take_v(1)
            normalise(4, *ln1)
            normalise(5, *ln1)
            take_context(0)
            take_embed(6)
            for r in range(4):
                mask_and_max(4 + r)
            take_oproj(0)
            take_oproj(1)
            take_k(2)
            normalise(6, *ln1)
            normalise(0, *ln2)
            normalise(1, *ln2)
            take_v(2)
            take_context(1)
            take_embed(7)
            for r in range(4):
                mask_and_max(8 + r)
            normalise(7, *ln1)
            take_oproj(2)
            take_oproj(3)
            take_logits(0)
            take_k(3)
            normalise(2, *ln2)
            normalise(3, *ln2)
            walk(0)
            coefficients(0, 1)
            take_context(2)
            take_v(3)
            for r in range(4):
                mask_and_max(12 + r)
            take_oproj(4)
            take_oproj(5)
            take_logits(1)
            take_leaf(0)
            take_leaf(1)
            walk(1)
            normalise(4, *ln2)
            normalise(5, *ln2)
            coefficients(1, 2)
            take_context(3)
            take_logits(2)
            walk(2)
            take_oproj(6)
            coefficients(2, 3)
            take_oproj(7)
            take_leaf(2)
            take_leaf(3)
            normalise(6, *ln2)
            normalise(7, *ln2)
            take_leaf(4)
            take_leaf(5)
            take_logits(3)
            walk(3)
            coefficients(3, 4)
            take_leaf(6)
            take_leaf(7)

        @block.tensor
        def _(pe):
            def bank_free(stage, g, n):
                user = previous_user(stage, g, n)
                if user is None:
                    return
                name, ug = user
                if name == "scores":
                    pe.wait_ge(masked, ug + 1)
                elif name == "probsT":
                    pe.wait_ge(pT_done, PT_BANKS * ug + n + 1)
                elif name == "qk":
                    pe.wait_ge(*((qk_done, 4 * (ug + 1)) if n == 7 else (k_done, 2 * (ug + 1))))
                elif name == "context":
                    pe.wait_ge(cx_done, TPG * ug + n - 4 + 1)
                elif name in READ_BY_TILE:
                    pe.wait_ge(READ_BY_TILE[name], ug + 1)
                else:
                    reader, n_steps = READ_BY_GROUP[name]
                    pe.wait_ge(reader, n_steps * (ug + 1))

            def embed_step(t, k):
                g, half = divmod(t, TPG)
                return nc.tensor.matmul(bank[banks_of("embed", t)[0]][:, 0:D], pix[:, g, k, half * P:(half + 1) * P],
                                        wemb[:, k, :], start=(k == 0), stop=(k == KT - 1))

            def embed_first():
                for k in range(KT):
                    if k % 2 == 0:
                        pe.wait_ge(ld_first[k // 2], 32)
                    for t in range(TPG):
                        last = embed_step(t, k)
                        if k == KT - 1:
                            last.then_inc(ready["embed"], 1)

            def embed(t):
                bank_free("embed", t, banks_of("embed", t)[0])
                if t % TPG == 0:
                    pe.wait_ge(ld_pix[t // TPG], 16)
                for k in range(KT):
                    last = embed_step(t, k)
                last.then_inc(ready["embed"], 1)

            pe.wait_ge(warm_set, 1)
            for _ in range(WARM):
                nc.tensor.matmul(bank[7][:, :], warm[:, 0:P], warm[:, :], start=True, stop=True)
            embed_first()

            def transposes(t, stage, src, made):
                n = 6 + t % TPG
                bank_free(stage, t, n)
                if stage == "xnT" and t == 0:
                    pe.wait_ge(ld_const, 16)
                pe.wait_ge(made, t + 1)
                for j in range(2):
                    last = nc.tensor.transpose(bank[n][0:DH, j * P:(j + 1) * P],
                                               src[:, t % 4, j * DH:(j + 1) * DH], ident)
                last.then_inc(ready[stage], 1)

            def qk(g):
                if g == 0:
                    pe.wait_ge(ld_w, 16)
                pe.wait_ge(xnT_done, TPG * (g + 1))
                bank_free("qk", g, 7)
                for n, col, at in ((7, 0, 0), (7, 2 * P, GTOK), (6, P, 0)):
                    if n == 6:
                        bank_free("qk", g, 6)
                    for j in range(2):
                        last = nc.tensor.matmul(bank[n][:, at:at + GTOK], w[:, j, col:col + P], xnT[:, g % 2, j, :],
                                                start=(j == 0), stop=(j == 1))
                    if at or n == 6:
                        last.then_inc(ready["qk"], 1)

            def v(g):
                n, = banks_of("v", g)
                bank_free("v", g, n)
                for i in range(IPG):
                    for part in range(2):
                        for j in range(2):
                            col = W_V + j * HP * HD
                            last = nc.tensor.matmul(bank[n][j * T:(j + 1) * T, i * HP * HD:(i + 1) * HP * HD],
                                                    xnT[:, g % 2, part, i * T:(i + 1) * T],
                                                    w[:, part, col:col + HP * HD], start=(part == 0), stop=(part == 1))
                last.then_inc(ready["v"], 1)

            def scores(n):
                g, r = divmod(n, 4)
                bank_free("scores", n, r)
                if r == 0:
                    pe.wait_ge(qk_done, 4 * (g + 1))
                    pe.wait_ge(k_done, 2 * (g + 1))
                for hp in BANK_PAIRS[r]:
                    q, k = (q_a, k_a) if hp < 4 else (q_b, k_b)
                    rows = slice(32 * ROW_GROUP[hp], 32 * ROW_GROUP[hp] + 32)
                    for t in range(TPG):
                        col = (BLOCK[hp, t] - BANK_FIRST[r]) * P
                        for i in range(2):
                            im = 2 * t + i
                            last = nc.tensor.matmul(bank[r][i * T:(i + 1) * T, col:col + P],
                                                    q[rows, g % 2, im * T:(im + 1) * T],
                                                    k[rows, g % 2, im, :, :].rearrange("p j k -> p (j k)"),
                                                    start=True, stop=True)
                last.then_inc(ready["scores"], 1)

            def probsT(g):
                for r in range(PT_BANKS):
                    bank_free("probsT", g, r)
                    pe.wait_ge(exp_done, 4 * g + (2, 3, 4)[r])
                    for c in range(4):
                        last = nc.tensor.transpose(bank[r][:, c * P:(c + 1) * P], s[:, g % 2, 4 * r + c, :], ident)
                    last.then_inc(ready["probsT"], 1)

            def context(g):
                pe.wait_ge(v_done, 2 * (g + 1))
                for t in range(TPG):
                    bank_free("context", g, 4 + t)
                for n, (hp, t) in enumerate(BLOCKS):
                    if n % 4 == 0:
                        pe.wait_ge(pT_done, PT_BANKS * g + n // 4 + 1)
                    for i in range(2):
                        at = hp * 2 * VW
                        last = nc.tensor.matmul(bank[4 + t][i * T:(i + 1) * T, at:at + 2 * VW],
                                                pT[:, g % 2, n, i * T:(i + 1) * T],
                                                v_bd[:, g % 2, 2 * t + i, hp, :, :].rearrange("p j d -> p (j d)"),
                                                start=True, stop=True)
                    if n >= NBLK - TPG:
                        last.then_inc(ready["context"], 1)

            def weighted(dst, x, t, col, width):
                g, half = divmod(t, TPG)
                for j in range(2):
                    last = nc.tensor.matmul(dst, x[:, g % 2, j, half * P:(half + 1) * P], w[:, j, col:col + width],
                                            start=(j == 0), stop=(j == 1))
                return last

            def oproj(t):
                n = 4 + t % TPG
                bank_free("oproj", t, n)
                pe.wait_ge(cxT_done, t + 1)
                weighted(bank[n][:, 0:D], cxT, t, W_O, D).then_inc(ready["oproj"], 1)

            def logits(g):
                bank_free("logits", g, 6)
                pe.wait_ge(xfT_done, TPG * (g + 1))
                for half in range(TPG):
                    last = weighted(bank[6][:, half * NODES:(half + 1) * NODES], xfT, TPG * g + half, W_F, NODES)
                last.then_inc(ready["logits"], 1)

            def coefT(g):
                bank_free("coefT", g, 6)
                pe.wait_ge(coef_done, g + 1)
                for t in range(TPG):
                    last = nc.tensor.transpose(bank[6][0:CK, t * P:(t + 1) * P], coef[:, TPG * g + t, :], ident)
                last.then_inc(ready["coefT"], 1)

            def leaf(t):
                g, half = divmod(t, TPG)
                n, = banks_of("leaf", t)
                bank_free("leaf", t, n)
                if t == 0:
                    pe.wait_ge(ld_leaf, 16)
                pe.wait_ge(cT_done, g + 1)
                nc.tensor.matmul(bank[n][:, 0:D], cT[:, g % 2, half * P:(half + 1) * P], wleaf[:, :],
                                 start=True, stop=True).then_inc(ready["leaf"], 1)

            stages = {
                "embed": embed, "qk": qk, "v": v, "scores": scores, "probsT": probsT, "context": context,
                "coefT": coefT, "leaf": leaf, "oproj": oproj, "logits": logits,
                "xnT": lambda t: transposes(t, "xnT", xn, xn_done),
                "ctxT": lambda t: transposes(t, "ctxT", cx, cx_done),
                "xfT": lambda t: transposes(t, "xfT", xf, xf_done),
            }
            for stage, g in PE_ORDER[TPG:]:
                stages[stage](g)


def kernel(x, L0_tok_conv_w, L0_tok_conv_b, L0_tok_pos_table, L0_attn_w_q, L0_attn_b_q, L0_attn_w_k, L0_attn_b_k,
           L0_attn_w_v, L0_attn_b_v, L0_attn_w_o, L0_attn_b_o, L0_attn_bias_table, L0_ffn_weights_in,
           L0_ffn_weights_out):
    import numpy as np
    import concourse.bacc as bacc
    from concourse.bass_utils import run_bass_kernel_spmd as run

    px = np.asarray(x).reshape(B, C_IN, NP, PATCH, NP, PATCH).transpose(1, 3, 5, 0, 2, 4)
    px = px.reshape(KT, P, NG, GTOK).transpose(1, 2, 0, 3)
    we = np.asarray(L0_tok_conv_w).reshape(D, KT, P).transpose(2, 1, 0)
    def with_bias(w, b):
        return np.concatenate([np.asarray(w).T, np.asarray(b)[None, :]], axis=0)

    q, k, v, o = (with_bias(w, b) for w, b in ((L0_attn_w_q, L0_attn_b_q), (L0_attn_w_k, L0_attn_b_k),
                                               (L0_attn_w_v, L0_attn_b_v), (L0_attn_w_o, L0_attn_b_o)))
    f = with_bias(L0_ffn_weights_in, np.zeros(NODES, np.float32))
    v = v.reshape(D + 1, HP, 2, HD).transpose(0, 2, 1, 3).reshape(D + 1, D)
    w = np.concatenate([q[:, :P], k[:, :P], q[:, P:], k[:, P:], v, o, f], axis=1)
    proj = np.zeros((P, 2, W_END), np.float32)
    proj[:DH, 0], proj[:DH + 1, 1] = w[:DH], w[DH:]
    wo = np.asarray(L0_ffn_weights_out)
    step = POS_SIDE // NP
    pos = np.asarray(L0_tok_pos_table).reshape(NP, step, NP, step, D)[:, 0, :, 0].reshape(T, D)
    pos_conv = np.stack([np.concatenate([pos, pos]), np.broadcast_to(np.asarray(L0_tok_conv_b), (P, D))], axis=1)
    rel = np.arange(T)[:, None] - np.arange(T)[None, :] + MAX_REL
    win = np.asarray(L0_attn_bias_table)[rel]
    win = np.concatenate([win, win])
    head = (np.arange(P)[:, None] // HD) % 2 == np.arange(2)[None, :]
    constants = np.concatenate([np.eye(P), head], axis=1).astype(np.float32)

    host = dict(pixels=px, w_embed=we, w_proj=proj, w_leaf=np.concatenate([wo] + [wo[-1:]] * STAY + [np.zeros((P - CK, D), np.float32)]),
                pos_conv=pos_conv, bias_windows=win, constants=constants)
    nc = bacc.Bacc("TRN2", target_bir_lowering=False, num_devices=1)
    arrays, args = {}, []
    for name, a in host.items():
        arrays[name] = np.ascontiguousarray(a)
        args.append(nc.dram_tensor(name, a.shape, mybir.dt.from_np(a.dtype), kind="ExternalInput").ap())
    y = nc.dram_tensor("y_dram", (NT, P, D), mybir.dt.float32, kind="ExternalOutput").ap()
    vit_block(nc, *args, y)
    r = run(nc, [arrays], core_ids=[0])
    return r.results[0]["y_dram"].reshape(B, T, D)
```

```python
import concourse.bass as bass
from concourse import mybir
from contextlib import ExitStack

B, C_IN, SIDE, PATCH = 16, 3, 128, 16
NP = SIDE // PATCH
T = NP * NP
D, H = 192, 12
HD = D // H
K_PIX = C_IN * PATCH * PATCH
POS_SIDE = 32
MAX_REL = 128
NODES = 21
LAST = NODES - 1
DEPTH = 11
P = 128
NT = B * T // P
TPG = 2
NG = NT // TPG
GTOK = TPG * P
IPG = GTOK // T
KT = K_PIX // P
DH = D // 2
HP = H // 2
EPS = 1e-5
FIRST = (0, 1, 3)
PIX_LOADS = (1, 2, 3, 4, 6)
WARM = 3
N_SETUP = 10


def tree_steps():
    steps, walks = [], [((), 0)]
    for _ in range(1, DEPTH):
        further = []
        for path, node in walks:
            if 2 * node + 1 >= LAST:
                further.append((path, node, LAST))
            else:
                further += [(path + ((node, right),), node, 2 * node + 1 + right) for right in range(2)]
        steps += further
        walks = [(path, after) for path, _, after in further]
    return steps


STEPS = tree_steps()
NS = len(STEPS)

W_Q, W_K, W_QKB = 0, P, 2 * P
W_V = W_QKB + P
W_O = W_V + D
W_F = W_O + D
W_END = W_F + NS

QUADS = H // 4
BLOCKS = [(hp, t) for quad in range(QUADS) for t in range(TPG) for hp in (2 * quad, 2 * quad + 1)]
NBLK = len(BLOCKS)

PE_ORDER = [
    ("embed", 0), ("embed", 1), ("embed", 2), ("xnT", 0), ("xnT", 1), ("embed", 3), ("k", 0), ("v", 0),
    ("q", 0), ("qkb", 0), ("scores", 0), ("xnT", 2), ("embed", 4), ("scores", 1), ("xnT", 3), ("scores", 2),
    ("k", 1), ("v", 1), ("probsT", 0), ("embed", 5), ("qkb", 1), ("probsT", 1), ("q", 1), ("probsT", 2),
    ("embed", 6), ("context", 0), ("xnT", 4), ("scores", 3), ("context", 1), ("oproj", 0), ("scores", 4),
    ("xnT", 5), ("scores", 5), ("v", 2), ("oproj", 1), ("qkb", 2), ("embed", 7), ("k", 2), ("probsT", 3),
    ("q", 2), ("probsT", 4), ("probsT", 5), ("scores", 6), ("scores", 7), ("context", 2), ("context", 3),
    ("xnT", 6), ("xnT", 7), ("scores", 8), ("q", 3), ("oproj", 2), ("qkb", 3), ("oproj", 3), ("probsT", 6),
    ("xfT", 0), ("probsT", 7), ("k", 3), ("v", 3), ("scores", 9), ("probsT", 8), ("scores", 10),
    ("context", 4), ("logits", 0), ("scores", 11), ("xfT", 1), ("context", 5), ("oproj", 4), ("probsT", 9),
    ("logits", 1), ("turns", 0), ("probsT", 10), ("oproj", 5), ("xfT", 2), ("xfT", 3), ("turns", 1),
    ("probsT", 11), ("logits", 2), ("leaf", 0), ("context", 6), ("context", 7), ("turns", 2), ("logits", 3),
    ("oproj", 6), ("xfT", 4), ("oproj", 7), ("xfT", 5), ("logits", 4), ("leaf", 1), ("turns", 3), ("leaf", 2),
    ("turns", 4), ("xfT", 6), ("logits", 5), ("leaf", 3), ("leaf", 4), ("turns", 5), ("xfT", 7), ("logits", 6),
    ("logits", 7), ("turns", 6), ("leaf", 5), ("turns", 7), ("leaf", 6), ("leaf", 7),
]
BANKS = {
    "embed": (7, 2), "xnT": (6, 4), "xfT": (6, 3), "k": (5, 5), "q": (4, 4), "qkb": (3, 3), "v": (6, 6),
    "context": (2, 5), "oproj": (7, 5), "logits": (6, 3), "turns": (2, 7), "leaf": (5, 4),
}


def banks_of(stage, n):
    return n % QUADS if stage in ("scores", "probsT") else BANKS[stage][n % 2]


def previous_user(stage, n):
    at = PE_ORDER.index((stage, n))
    users = [x for x in PE_ORDER[:at] if banks_of(*x) == banks_of(stage, n)]
    return users[-1] if users else None


def vit_block(nc, first, pixels, w_proj, w_leaf, pos_conv, bias_windows, constants, out):
    f32 = mybir.dt.float32
    bf16 = mybir.dt.bfloat16
    ALU = mybir.AluOpType
    ACT = mybir.ActivationFunctionType
    AX = mybir.AxisListType

    ctx = ExitStack()
    with ctx:
        def sb(name, shape, dtype=f32):
            return ctx.enter_context(nc.sbuf_tensor(name, shape, dtype))

        def sem(name):
            return ctx.enter_context(nc.semaphore(name))

        weights_px0 = sb("weights_px0", [P, KT, D + P])
        pix = sb("pix", [P, NT, KT, P])
        w = sb("w", [P, 2, W_END])
        wleaf = sb("wleaf", [P, D])
        posc = sb("posc", [P, 2, D])
        windows = sb("windows", [P, T, H])
        const = sb("const", [P, P + 5 + NS])
        ident = const[:, 0:P]
        head_of_quad = const[:, P:P + 4]
        rights = const[:, P + 4:P + 5]
        pos = sb("pos", [P, D])
        mask = sb("mask", [P, T])
        mask_sum = sb("mask_sum", [P, T])
        warm = sb("warm", [P, 2 * P])
        neg_half = sb("neg_half", [P, 1])
        h = sb("h", [P, NT, D])
        h2 = sb("h2", [P, NT, D])
        stats = sb("stats", [P, NT, 6])
        mv = sb("mv", [P, NT, 2])
        var = sb("var", [P, NT])
        rstd = sb("rstd", [P, NT])
        stats_f = sb("stats_f", [P, NT, 6])
        mv_f = sb("mv_f", [P, NT, 2])
        var_f = sb("var_f", [P, NT])
        rstd_f = sb("rstd_f", [P, NT])
        xn = sb("xn", [P, NT, D])
        xnT = sb("xnT", [P, 2, 2, GTOK])
        q_a = sb("q_a", [P, NG, GTOK])
        q_b = sb("q_b", [P, NG, GTOK])
        k_a = sb("k_a", [P, NG, IPG, 4, T])
        k_b = sb("k_b", [P, NG, IPG, 4, T])
        v_bd = sb("v_bd", [P, 2, IPG, HP, 2, HD])
        s = sb("s", [P, NG, NBLK, 2 * T])
        smax = sb("smax", [P, NG, NBLK, 2])
        ssum = sb("ssum", [P, NG, NBLK, 2])
        rsum = sb("rsum", [P, NG, NBLK, 2])
        pT = sb("pT", [P, NG, NBLK, P])
        cxT = sb("cxT", [P, 2, 2, GTOK])
        xf = sb("xf", [P, NT, D])
        xfT = sb("xfT", [P, 2, 2, GTOK])
        right = sb("right", [P, 4, P], bf16)
        paths = sb("paths", [P, NS], bf16)
        gel = sb("gel", [P, NT, P])
        cT = sb("cT", [P, 4, P])
        y = sb("y", [P, NT, D])

        bank = [ctx.enter_context(nc.psum_tensor(f"bank{n}", [P, 512], f32)) for n in range(8)]

        ld_first = {k: sem(f"ld_first{k}") for k in FIRST}
        ld_pix = {t: sem(f"ld_pix{t}") for t in PIX_LOADS}
        ld_const = sem("ld_const")
        ld_pos = sem("ld_pos")
        ld_win = sem("ld_win")
        ld_w = sem("ld_w")
        ld_leaf = sem("ld_leaf")
        stored = sem("stored")
        ready = {x: sem("pe_" + x) for x in sorted({x[0] for x in PE_ORDER})}
        setup = sem("setup")
        warm_set = sem("warm_set")
        paths_set = sem("paths_set")
        h_done = sem("h_done")
        var_done = sem("var_done")
        rstd_done = sem("rstd_done")
        xn_done = sem("xn_done")
        xnT_done = sem("xnT_done")
        q_done = sem("q_done")
        k_done = sem("k_done")
        qkb_done = sem("qkb_done")
        v_done = sem("v_done")
        masked = sem("masked")
        max_done = sem("max_done")
        shifted = sem("shifted")
        exp_done = sem("exp_done")
        sum_done = sem("sum_done")
        scaled = sem("scaled")
        pT_done = sem("pT_done")
        cxT_done = sem("cxT_done")
        h2_done = sem("h2_done")
        varf_done = sem("varf_done")
        rstdf_done = sem("rstdf_done")
        xf_done = sem("xf_done")
        xfT_done = sem("xfT_done")
        right_done = sem("right_done")
        gel_done = sem("gel_done")
        coef_done = sem("coef_done")
        y_done = sem("y_done")
        dve_step = sem("dve_step")

        READ = {"embed": (h_done, 1), "xnT": (xnT_done, 1), "q": (q_done, 1), "k": (k_done, 1), "qkb": (qkb_done, 5),
                "v": (v_done, 4), "scores": (masked, 1), "probsT": (pT_done, 1), "context": (cxT_done, 1),
                "oproj": (h2_done, 1), "xfT": (xfT_done, 1), "logits": (gel_done, 1),
                "turns": (coef_done, 1), "leaf": (y_done, 1)}

        units = 4 * TPG

        def score_rows(n):
            g, r = divmod(n, QUADS)
            return s[:, g, 4 * r:4 * r + 4, :].rearrange("p a (j k) -> p (a j) k", j=2)

        def row_values(x, n):
            g, r = divmod(n, QUADS)
            return x[:, g, 4 * r:4 * r + 4, :].rearrange("p a j -> p (a j)")

        def for_keys(values):
            return values.unsqueeze(2).to_broadcast([P, units, T])

        block = ctx.enter_context(nc.Block())

        @block.sync
        def _(sp):
            for k, end in zip(FIRST[::2], (FIRST + (KT,))[1::2]):
                sp.dma_start(weights_px0[:, k:end, :], first[:, k:end, :]).then_inc(ld_first[k], 16)
            sp.dma_start(posc[:, :, :], pos_conv).then_inc(ld_pos, 16)
            sp.dma_start(pix[:, 2, :, :], pixels[:, 2, :, :]).then_inc(ld_pix[2], 16)
            sp.dma_start(pix[:, 3, :, :], pixels[:, 3, :, :]).then_inc(ld_pix[3], 16)
            sp.dma_start(w[:, :, :], w_proj).then_inc(ld_w, 16)
            sp.dma_start(windows[:, :, :], bias_windows).then_inc(ld_win, 16)
            sp.dma_start(pix[:, 4:6, :, :], pixels[:, 4:6, :, :]).then_inc(ld_pix[4], 16)
            sp.dma_start(pix[:, 6:8, :, :], pixels[:, 6:8, :, :]).then_inc(ld_pix[6], 16)
            sp.dma_start(wleaf[:, :], w_leaf).then_inc(ld_leaf, 16)
            for t in range(NT):
                sp.wait_ge(y_done, t + 1)
                sp.dma_start(out[t, :, :], y[:, t, :]).then_inc(stored, 16)
            sp.wait_ge(stored, 16 * NT)

        @block.gpsimd
        def _(pool):
            n_set = 0
            for view, value in (
                (neg_half[:, :], -0.5),
                (right[:, :, :], 0.0),
                (xnT[DH:P, :, :, :], 0.0), (cxT[DH:P, :, :, :], 0.0), (xfT[DH:P, :, :, :], 0.0),
                (xnT[DH:DH + 1, :, 1, :], 1.0), (cxT[DH:DH + 1, :, 1, :], 1.0), (xfT[DH:DH + 1, :, 1, :], 1.0),
                (v_bd[0:T, :, :, :, 1, :], 0.0), (v_bd[T:P, :, :, :, 0, :], 0.0),
            ):
                if n_set:
                    pool.wait_ge(setup, n_set)
                nc.gpsimd.memset(view, value).then_inc(setup, 1)
                n_set += 1

            def root(t, vs, rs, var_sem, rstd_sem):
                pool.wait_ge(var_sem, t + 1)
                if t == 0:
                    pool.wait_ge(setup, N_SETUP)
                nc.gpsimd.tensor_tensor(rs[:, t:t + 1], vs[:, t:t + 1], neg_half[:, :], ALU.pow).then_inc(rstd_sem, 1)

            def shift(n):
                rows = score_rows(n)
                pool.wait_ge(max_done, n + 1)
                nc.gpsimd.tensor_tensor(rows, rows, for_keys(row_values(smax, n)), ALU.subtract)\
                    .then_inc(shifted, 1)

            def scale(n):
                rows = score_rows(n)
                pool.wait_ge(sum_done, n + 1)
                nc.gpsimd.tensor_tensor(rows, rows, for_keys(row_values(rsum, n)), ALU.mult).then_inc(scaled, 1)

            ln1 = (var, rstd, var_done, rstd_done)
            ln2 = (var_f, rstd_f, varf_done, rstdf_done)
            root(0, *ln1)
            root(1, *ln1)
            root(2, *ln1)
            root(3, *ln1)
            shift(0)
            root(4, *ln1)
            scale(0)
            shift(1)
            shift(2)
            scale(1)
            scale(2)
            root(5, *ln1)
            shift(3)
            root(0, *ln2)
            shift(4)
            scale(3)
            shift(5)
            scale(4)
            root(6, *ln1)
            scale(5)
            root(7, *ln1)
            shift(6)
            shift(7)
            root(1, *ln2)
            scale(6)
            shift(8)
            scale(7)
            root(2, *ln2)
            scale(8)
            shift(9)
            shift(10)
            scale(9)
            root(3, *ln2)
            shift(11)
            scale(10)
            scale(11)
            root(4, *ln2)
            root(5, *ln2)
            root(6, *ln2)
            root(7, *ln2)

        @block.scalar
        def _(act):
            act.dma_start(weights_px0[:, FIRST[1]:FIRST[2], :], first[:, FIRST[1]:FIRST[2], :])\
                .then_inc(ld_first[FIRST[1]], 16)
            act.dma_start(pix[:, 1, :, :], pixels[:, 1, :, :]).then_inc(ld_pix[1], 16)
            act.dma_start(const[:, :], constants).then_inc(ld_const, 16)

            def copy_T(t, stage, dst, done):
                g, half = divmod(t, TPG)
                act.wait_ge(ready[stage], t + 1)
                nc.scalar.activation(dst[0:DH, g % 2, :, half * P:(half + 1) * P],
                                     bank[banks_of(stage, t)][0:DH, 0:2 * P].rearrange("p (j n) -> p j n", j=2),
                                     ACT.Copy).then_inc(done, 1)

            def copy_q(g):
                act.wait_ge(ready["q"], g + 1)
                nc.scalar.activation(q_a[:, g, :], bank[banks_of("q", g)][:, 0:GTOK], ACT.Copy, scale=HD ** -0.5)\
                    .then_inc(q_done, 1)

            def copy_qkb(g):
                if g == 0:
                    act.wait_ge(ld_const, 16)
                act.wait_ge(ready["qkb"], g + 1)
                n = banks_of("qkb", g)
                nc.scalar.activation(q_b[T:P, g, :], bank[n][0:T, 0:GTOK], ACT.Copy, scale=HD ** -0.5)\
                    .then_inc(qkb_done, 1)
                for j in range(4):
                    src = bank[n][T:P, 0:GTOK].rearrange("p (i k) -> p i k", i=IPG)
                    nc.scalar.activation(k_b[T:P, g, :, j, :], src, ACT.Copy,
                                         scale=head_of_quad[T:P, j:j + 1]).then_inc(qkb_done, 1)

            def copy_v(g):
                act.wait_ge(ready["v"], g + 1)
                src = bank[banks_of("v", g)][:, 0:TPG * D].rearrange("p (t j a d) -> p t j a d", t=TPG, j=2, a=HP)
                dst = v_bd[:, g % 2, :, :, :, :].rearrange("p (t i) a j d -> p t i a j d", t=TPG)
                for i in range(2):
                    for j in range(2):
                        nc.scalar.activation(dst[j * T:(j + 1) * T, :, i, :, j, :],
                                             src[i * T:(i + 1) * T, :, j, :, :], ACT.Copy).then_inc(v_done, 1)

            def exp(n):
                rows = score_rows(n)
                act.wait_ge(shifted, n + 1)
                nc.scalar.activation(rows, rows, ACT.Exp).then_inc(exp_done, 1)

            def copy_pT(n):
                g, r = divmod(n, QUADS)
                act.wait_ge(ready["probsT"], n + 1)
                nc.scalar.activation(pT[:, g, 4 * r:4 * r + 4, :].rearrange("p a b -> p (a b)"), bank[r][:, :],
                                     ACT.Copy).then_inc(pT_done, 1)

            def copy_xnT(t):
                copy_T(t, "xnT", xnT, xnT_done)

            def copy_context(t):
                copy_T(t, "context", cxT, cxT_done)

            def copy_xfT(t):
                copy_T(t, "xfT", xfT, xfT_done)

            def gelu(t):
                act.wait_ge(right_done, t + 1)
                nc.scalar.activation(gel[0:NS, t, :], bank[banks_of("logits", t)][0:NS, 0:P], ACT.Gelu)\
                    .then_inc(gel_done, 1)

            act.wait_ge(setup, N_SETUP)
            copy_xnT(0)
            copy_xnT(1)
            copy_v(0)
            copy_q(0)
            copy_qkb(0)
            copy_xnT(2)
            exp(0)
            copy_xnT(3)
            exp(1)
            exp(2)
            copy_v(1)
            copy_pT(0)
            copy_qkb(1)
            copy_pT(1)
            copy_q(1)
            copy_pT(2)
            copy_xnT(4)
            copy_context(0)
            copy_xnT(5)
            exp(3)
            copy_context(1)
            exp(4)
            exp(5)
            copy_pT(3)
            copy_q(2)
            copy_pT(4)
            copy_pT(5)
            copy_qkb(2)
            copy_v(2)
            copy_context(2)
            exp(6)
            copy_xnT(6)
            copy_xnT(7)
            copy_context(3)
            exp(7)
            exp(8)
            copy_q(3)
            copy_xfT(0)
            copy_qkb(3)
            copy_pT(6)
            copy_v(3)
            copy_pT(7)
            copy_pT(8)
            copy_context(4)
            exp(9)
            copy_context(5)
            exp(10)
            copy_pT(9)
            copy_xfT(1)
            exp(11)
            gelu(0)
            gelu(1)
            copy_xfT(2)
            copy_pT(10)
            copy_pT(11)
            gelu(2)
            copy_xfT(3)
            copy_context(6)
            copy_context(7)
            copy_xfT(4)
            gelu(3)
            copy_xfT(5)
            gelu(4)
            gelu(5)
            copy_xfT(6)
            copy_xfT(7)
            gelu(6)
            gelu(7)

        @block.vector
        def _(dve):
            chain = [0]

            def link(ins):
                chain[0] += 1
                ins.then_inc(dve_step, 1)
                dve.wait_ge(dve_step, chain[0])

            def mark(ins):
                chain[0] += 1
                ins.then_inc(dve_step, 1)

            def hold():
                dve.wait_ge(dve_step, chain[0])

            nc.vector.memset(warm[:, :], 0.0).then_inc(warm_set, 1)
            mark(nc.vector.memset(cT[:, :, :], 0.0))
            dve.wait_ge(ld_pos, 16)
            link(nc.vector.tensor_tensor(pos[:, :], posc[:, 0, :], posc[:, 1, :], ALU.add))

            def variance(t, x, st, mvs, vs, done):
                link(nc.vector.bn_stats(st[:, t, :], x[:, t, :]))
                link(nc.vector.bn_aggr(mvs[:, t, :], st[:, t, :]))
                nc.vector.tensor_single_scalar(vs[:, t:t + 1], mvs[:, t, 1:2], EPS, ALU.add).then_inc(done, 1)

            def normalise(t, x, mvs, rs, dst, rstd_sem, done):
                dve.wait_ge(rstd_sem, t + 1)
                nc.vector.tensor_scalar(dst[:, t, :], x[:, t, :], mvs[:, t, 0:1], rs[:, t:t + 1],
                                        ALU.subtract, ALU.mult).then_inc(done, 1)

            def take_embed(t):
                dve.wait_ge(ready["embed"], t + 1)
                nc.vector.tensor_tensor(h[:, t, :], bank[banks_of("embed", t)][:, 0:D], pos[:, :], ALU.add)\
                    .then_inc(h_done, 1)
                dve.wait_ge(h_done, t + 1)
                variance(t, h, stats, mv, var, var_done)

            def take_k(g):
                dve.wait_ge(ready["k"], g + 1)
                if g == 0:
                    dve.wait_ge(ld_const, 16)
                shape = [P, IPG, 4, T]
                src = bank[banks_of("k", g)][:, 0:GTOK].rearrange("p (i k) -> p i k", i=IPG)
                nc.vector.tensor_tensor(k_a[:, g, :, :, :], src.unsqueeze(2).to_broadcast(shape),
                                        head_of_quad.unsqueeze(1).unsqueeze(3).to_broadcast(shape), ALU.mult)\
                    .then_inc(k_done, 1)

            def mask_and_max(n):
                rows = score_rows(n)
                if n == 0:
                    hold()
                dve.wait_ge(ready["scores"], n + 1)
                nc.vector.tensor_tensor(rows, bank[banks_of("scores", n)][:, :].rearrange("p (u k) -> p u k", k=T),
                                        mask[:, :].unsqueeze(1).to_broadcast([P, units, T]), ALU.add)\
                    .then_inc(masked, 1)
                dve.wait_ge(masked, n + 1)
                nc.vector.tensor_reduce(row_values(smax, n), rows, AX.X, ALU.max).then_inc(max_done, 1)

            def sums(n):
                dve.wait_ge(exp_done, n + 1)
                link(nc.vector.tensor_reduce(row_values(ssum, n), score_rows(n), AX.X, ALU.add))
                nc.vector.reciprocal(row_values(rsum, n), row_values(ssum, n)).then_inc(sum_done, 1)

            def take_oproj(t):
                dve.wait_ge(ready["oproj"], t + 1)
                nc.vector.tensor_tensor(h2[:, t, :], bank[banks_of("oproj", t)][:, 0:D], h[:, t, :], ALU.add)\
                    .then_inc(h2_done, 1)
                dve.wait_ge(h2_done, t + 1)
                variance(t, h2, stats_f, mv_f, var_f, varf_done)

            def take_logits(t):
                dve.wait_ge(ready["logits"], t + 1)
                nc.vector.tensor_single_scalar(right[0:NS, t % 4, :], bank[banks_of("logits", t)][0:NS, 0:P], 0.0,
                                               ALU.is_gt).then_inc(right_done, 1)

            def coefficients(t):
                if t == 0:
                    hold()
                dve.wait_ge(ready["turns"], t + 1)
                dve.wait_ge(gel_done, t + 1)
                nc.vector.scalar_tensor_tensor(cT[0:NS, t % 4, :], bank[banks_of("turns", t)][0:NS, 0:P],
                                               rights[0:NS, :], gel[0:NS, t, :], ALU.is_equal, ALU.mult)\
                    .then_inc(coef_done, 1)

            def take_leaf(t):
                dve.wait_ge(ready["leaf"], t + 1)
                nc.vector.tensor_tensor(y[:, t, :], bank[banks_of("leaf", t)][:, 0:D], h2[:, t, :], ALU.add)\
                    .then_inc(y_done, 1)

            def make_mask():
                dve.wait_ge(ld_const, 16)
                nc.vector.tensor_copy(paths[:, :], const[:, P + 5:]).then_inc(paths_set, 1)
                dve.wait_ge(ld_win, 16)
                link(nc.vector.tensor_reduce(mask_sum[:, :], windows[:, :, :], AX.X, ALU.add))
                mark(nc.vector.tensor_single_scalar(mask[:, :], mask_sum[:, :], 1.0 / H, ALU.mult))

            ln1 = (h, mv, rstd, xn, rstd_done, xn_done)
            ln2 = (h2, mv_f, rstd_f, xf, rstdf_done, xf_done)
            take_embed(0)
            take_embed(1)
            normalise(0, *ln1)
            normalise(1, *ln1)
            take_embed(2)
            make_mask()
            take_embed(3)
            normalise(2, *ln1)
            take_k(0)
            normalise(3, *ln1)
            mask_and_max(0)
            take_embed(4)
            sums(0)
            mask_and_max(1)
            mask_and_max(2)
            normalise(4, *ln1)
            sums(1)
            sums(2)
            take_embed(5)
            take_k(1)
            take_embed(6)
            normalise(5, *ln1)
            mask_and_max(3)
            take_oproj(0)
            mask_and_max(4)
            sums(3)
            mask_and_max(5)
            take_oproj(1)
            sums(4)
            sums(5)
            take_embed(7)
            take_k(2)
            normalise(6, *ln1)
            normalise(7, *ln1)
            mask_and_max(6)
            mask_and_max(7)
            normalise(0, *ln2)
            sums(6)
            mask_and_max(8)
            sums(7)
            take_oproj(2)
            take_oproj(3)
            sums(8)
            take_k(3)
            mask_and_max(9)
            mask_and_max(10)
            normalise(1, *ln2)
            sums(9)
            mask_and_max(11)
            take_logits(0)
            sums(10)
            take_oproj(4)
            sums(11)
            normalise(2, *ln2)
            take_logits(1)
            normalise(3, *ln2)
            coefficients(0)
            take_oproj(5)
            coefficients(1)
            take_logits(2)
            take_leaf(0)
            normalise(4, *ln2)
            coefficients(2)
            normalise(5, *ln2)
            take_logits(3)
            take_oproj(6)
            take_oproj(7)
            take_logits(4)
            normalise(6, *ln2)
            take_leaf(1)
            take_leaf(2)
            coefficients(3)
            coefficients(4)
            take_logits(5)
            normalise(7, *ln2)
            coefficients(5)
            take_leaf(3)
            take_logits(6)
            take_leaf(4)
            take_logits(7)
            coefficients(6)
            take_leaf(5)
            coefficients(7)
            take_leaf(6)
            take_leaf(7)

        @block.tensor
        def _(pe):
            def bank_free(stage, n):
                user = previous_user(stage, n)
                if user is not None:
                    reader, times = READ[user[0]]
                    pe.wait_ge(reader, times * (user[1] + 1))
                return bank[banks_of(stage, n)]

            def embed(t):
                dst = bank_free("embed", t)
                if t in PIX_LOADS:
                    pe.wait_ge(ld_pix[t], 16)
                for k in range(KT):
                    if t == 0 and k in FIRST:
                        pe.wait_ge(ld_first[k], 16)
                    px = weights_px0[:, k, D:D + P] if t == 0 else pix[:, t, k, :]
                    last = nc.tensor.matmul(dst[:, 0:D], px, weights_px0[:, k, 0:D], start=(k == 0),
                                            stop=(k == KT - 1))
                last.then_inc(ready["embed"], 1)

            def transposes(t, stage, src, made):
                dst = bank_free(stage, t)
                if stage == "xnT" and t == 0:
                    pe.wait_ge(ld_const, 16)
                pe.wait_ge(made, t + 1)
                for j in range(2):
                    last = nc.tensor.transpose(dst[0:DH, j * P:(j + 1) * P],
                                               src[:, t, j * DH:(j + 1) * DH], ident)
                last.then_inc(ready[stage], 1)

            def projection(stage, g, col):
                if g == 0:
                    pe.wait_ge(ld_w, 16)
                pe.wait_ge(xnT_done, TPG * (g + 1))
                dst = bank_free(stage, g)
                for j in range(2):
                    last = nc.tensor.matmul(dst[:, 0:GTOK], w[:, j, col:col + P], xnT[:, g % 2, j, :],
                                            start=(j == 0), stop=(j == 1))
                last.then_inc(ready[stage], 1)

            def v(g):
                if g == 0:
                    pe.wait_ge(ld_w, 16)
                pe.wait_ge(xnT_done, TPG * (g + 1))
                dst = bank_free("v", g)
                for t in range(TPG):
                    for part in range(2):
                        last = nc.tensor.matmul(dst[:, t * D:(t + 1) * D], xnT[:, g % 2, part, t * P:(t + 1) * P],
                                                w[:, part, W_V:W_V + D], start=(part == 0), stop=(part == 1))
                last.then_inc(ready["v"], 1)

            def scores(n):
                g, quad = divmod(n, QUADS)
                dst = bank_free("scores", n)
                if quad < 2:
                    pe.wait_ge(q_done, g + 1)
                    pe.wait_ge(k_done, g + 1)
                else:
                    pe.wait_ge(qkb_done, 5 * (g + 1))
                q, k = (q_a, k_a) if quad < 2 else (q_b, k_b)
                rows = slice(0, T) if quad == 0 else slice(T, P)
                for t in range(TPG):
                    for i in range(2):
                        im = 2 * t + i
                        last = nc.tensor.matmul(dst[i * T:(i + 1) * T, t * 4 * T:(t + 1) * 4 * T],
                                                q[rows, g, im * T:(im + 1) * T],
                                                k[rows, g, im, :, :].rearrange("p j k -> p (j k)"),
                                                start=True, stop=True)
                last.then_inc(ready["scores"], 1)

            def probsT(n):
                g, r = divmod(n, QUADS)
                dst = bank_free("probsT", n)
                pe.wait_ge(scaled, n + 1)
                for c in range(4):
                    last = nc.tensor.transpose(dst[:, c * P:(c + 1) * P], s[:, g, 4 * r + c, :], ident)
                last.then_inc(ready["probsT"], 1)

            def context(t):
                g, tile = divmod(t, TPG)
                dst = bank_free("context", t)
                pe.wait_ge(v_done, 4 * (g + 1))
                pe.wait_ge(pT_done, QUADS * (g + 1))
                for i in range(2):
                    for hp in range(HP):
                        half, at = divmod(hp, HP // 2)
                        rows = slice(at * 2 * HD, (at + 1) * 2 * HD)
                        last = nc.tensor.matmul(dst[rows, half * P + i * T:half * P + (i + 1) * T],
                                                v_bd[:, g % 2, 2 * tile + i, hp, :, :].rearrange("p j d -> p (j d)"),
                                                pT[:, g, BLOCKS.index((hp, tile)), i * T:(i + 1) * T],
                                                start=True, stop=True)
                last.then_inc(ready["context"], 1)

            def oproj(t):
                g, half = divmod(t, TPG)
                dst = bank_free("oproj", t)
                pe.wait_ge(cxT_done, t + 1)
                for j in range(2):
                    last = nc.tensor.matmul(dst[:, 0:D], cxT[:, g % 2, j, half * P:(half + 1) * P],
                                            w[:, j, W_O:W_O + D], start=(j == 0), stop=(j == 1))
                last.then_inc(ready["oproj"], 1)

            def logits(t):
                g, half = divmod(t, TPG)
                dst = bank_free("logits", t)
                pe.wait_ge(xfT_done, t + 1)
                for j in range(2):
                    last = nc.tensor.matmul(dst[0:NS, 0:P], w[:, j, W_F:W_F + NS],
                                            xfT[:, g % 2, j, half * P:(half + 1) * P], start=(j == 0), stop=(j == 1))
                last.then_inc(ready["logits"], 1)

            def turns(t):
                dst = bank_free("turns", t)
                if t == 0:
                    pe.wait_ge(paths_set, 1)
                pe.wait_ge(right_done, t + 1)
                nc.tensor.matmul(dst[0:NS, 0:P], paths[:, :], right[:, t % 4, :], start=True, stop=True)\
                    .then_inc(ready["turns"], 1)

            def leaf(t):
                dst = bank_free("leaf", t)
                if t == 0:
                    pe.wait_ge(ld_leaf, 16)
                pe.wait_ge(coef_done, t + 1)
                nc.tensor.matmul(dst[:, 0:D], cT[:, t % 4, :], wleaf[:, :], start=True, stop=True)\
                    .then_inc(ready["leaf"], 1)

            stages = {
                "embed": embed, "v": v, "scores": scores, "probsT": probsT, "context": context,
                "turns": turns, "leaf": leaf, "oproj": oproj, "logits": logits,
                "q": lambda g: projection("q", g, W_Q), "k": lambda g: projection("k", g, W_K),
                "qkb": lambda g: projection("qkb", g, W_QKB),
                "xnT": lambda t: transposes(t, "xnT", xn, xn_done),
                "xfT": lambda t: transposes(t, "xfT", xf, xf_done),
            }
            pe.wait_ge(warm_set, 1)
            for _ in range(WARM):
                nc.tensor.matmul(bank[7][:, 0:2 * P], warm[:, 0:P], warm[:, :], start=True, stop=True)
            for stage, g in PE_ORDER:
                stages[stage](g)


def kernel(x, L0_tok_conv_w, L0_tok_conv_b, L0_tok_pos_table, L0_attn_w_q, L0_attn_b_q, L0_attn_w_k, L0_attn_b_k,
           L0_attn_w_v, L0_attn_b_v, L0_attn_w_o, L0_attn_b_o, L0_attn_bias_table, L0_ffn_weights_in,
           L0_ffn_weights_out):
    import numpy as np
    import concourse.bacc as bacc
    from concourse.bass_utils import run_bass_kernel_spmd as run

    px = np.asarray(x).reshape(B, C_IN, NP, PATCH, NP, PATCH).transpose(1, 3, 5, 0, 2, 4)
    px = px.reshape(KT, P, NT, P).transpose(1, 2, 0, 3)
    we = np.asarray(L0_tok_conv_w).reshape(D, KT, P).transpose(2, 1, 0)

    def with_bias(w, b):
        return np.concatenate([np.asarray(w).T, np.asarray(b)[None, :]], axis=0)

    q, k, v, o = (with_bias(w, b) for w, b in ((L0_attn_w_q, L0_attn_b_q), (L0_attn_w_k, L0_attn_b_k),
                                               (L0_attn_w_v, L0_attn_b_v), (L0_attn_w_o, L0_attn_b_o)))
    nodes = [node for _, node, _ in STEPS]
    f = with_bias(L0_ffn_weights_in, np.zeros(NODES, np.float32))[:, nodes]
    v = v.reshape(D + 1, HP, 2, HD).transpose(0, 2, 1, 3).reshape(D + 1, D)
    w = np.concatenate([q[:, :P], k[:, :P], q[:, P:], k[:, P:], v, o, f], axis=1)
    proj = np.zeros((P, 2, W_END), np.float32)
    proj[:DH, 0], proj[:DH + 1, 1] = w[:DH], w[DH:]
    leaf = np.zeros((P, D), np.float32)
    leaf[:NS] = np.asarray(L0_ffn_weights_out)[[after for _, _, after in STEPS]]
    step = POS_SIDE // NP
    pos = np.asarray(L0_tok_pos_table).reshape(NP, step, NP, step, D)[:, 0, :, 0].reshape(T, D)
    pos_conv = np.stack([np.concatenate([pos, pos]), np.broadcast_to(np.asarray(L0_tok_conv_b), (P, D))], axis=1)
    rel = np.arange(T)[:, None] - np.arange(T)[None, :] + MAX_REL
    win = np.asarray(L0_attn_bias_table)[rel]
    win = np.concatenate([win, win])
    head = (np.arange(P)[:, None] // HD) % 4 == np.arange(4)[None, :]
    rights, paths = np.zeros((P, 1)), np.zeros((P, NS))
    for n, (path, _, _) in enumerate(STEPS):
        for node, right in path:
            paths[nodes.index(node), n] = 1 if right else -1
            rights[n] += right
    constants = np.concatenate([np.eye(P), head, rights, paths], axis=1).astype(np.float32)

    host = dict(first=np.concatenate([we, px[:, 0]], axis=2), pixels=px, w_proj=proj, w_leaf=leaf,
                pos_conv=pos_conv, bias_windows=win, constants=constants)
    nc = bacc.Bacc("TRN2", target_bir_lowering=False, num_devices=1)
    arrays, args = {}, []
    for name, a in host.items():
        arrays[name] = np.ascontiguousarray(a)
        args.append(nc.dram_tensor(name, a.shape, mybir.dt.from_np(a.dtype), kind="ExternalInput").ap())
    y = nc.dram_tensor("y_dram", (NT, P, D), mybir.dt.float32, kind="ExternalOutput").ap()
    vit_block(nc, *args, y)
    r = run(nc, [arrays], core_ids=[0])
    return r.results[0]["y_dram"].reshape(B, T, D)
```
